# Optimizing a Trainium2 kernel written in Bass

```python
import numpy as np
import jax
import jax.numpy as jnp

def _softmax(x, axis=-1):
    return jax.nn.softmax(x, axis=axis)

def _gelu(x):
    return jax.nn.gelu(x, approximate=True)

def _silu(x):
    return jax.nn.silu(x)

def _sigmoid(x):
    return jax.nn.sigmoid(x)

def _layernorm(x, axis=-1, eps=1e-05):
    m = jnp.mean(x, axis=axis, keepdims=True)
    v = jnp.var(x, axis=axis, keepdims=True)
    return (x - m) / jnp.sqrt(v + eps)

def _scatter_add(tgt, idx, src, axis=0):
    return tgt.at[idx].add(src)

def _segment_sum(src, seg, n):
    return jax.ops.segment_sum(src, seg, n)
kernel_name = 'mk_xattn_ffn_d1_seqx_r8_3e4707'

def setup_inputs(seed: int=0):
    np.random.seed(seed)
    _w = jnp.asarray

    def _rec_inputs():
        import jax
        import jax.numpy as jnp
        _rk = jax.random.key(seed)
        x = -0.0003929 + 0.9999 * jax.random.normal(jax.random.fold_in(_rk, 1), (32, 64, 512), jnp.float32)
        _lenS = 64 - jax.random.randint(jax.random.fold_in(_rk, 7), (32,), 0, max(1, 64 // 4) + 1, jnp.int32)
        _lenS2 = 64 - jax.random.randint(jax.random.fold_in(_rk, 8), (32,), 0, max(1, 64 // 4) + 1, jnp.int32)
        _ctx_4096P = jax.random.normal(jax.random.fold_in(_rk, 11), (32, 16, 512), jnp.float32)
        _ctx_4096c = jax.random.dirichlet(jax.random.fold_in(_rk, 511), 0.3 * jnp.ones((16,), jnp.float32), (32, 64))
        _ctx_4096t = jnp.einsum('bsk,bkd->bsd', _ctx_4096c, _ctx_4096P)
        _ctx_4096t = _ctx_4096t * jax.lax.rsqrt(jnp.mean(jnp.square(_ctx_4096t)) + 1e-12) * 0.953939
        ctx_4096 = 2.81802e-05 + 1.00001 * (_ctx_4096t + 0.3 * jax.random.normal(jax.random.fold_in(_rk, 611), (32, 64, 512), jnp.float32))
        pos_BxS2 = jnp.broadcast_to(jnp.arange(64, dtype=jnp.int32), (32, 64))
        _validS = jnp.arange(64)[None, :] < _lenS[:, None]
        _validS2 = jnp.arange(64)[None, :] < _lenS2[:, None]
        _causal = jnp.tril(jnp.ones((64, 64), dtype=bool))
        mask_BxSxS2_ik0 = jnp.where(jnp.broadcast_to(_validS2[:, None, :], (32, 64, 64)), 0, 1).astype(jnp.int32)
        return (x, ctx_4096, pos_BxS2, mask_BxSxS2_ik0)
    x, ctx_4096, pos_BxS2, mask_BxSxS2_ik0 = _rec_inputs()

    def _L0_xattn_setup():
        import jax, jax.numpy as jnp
        import numpy as np
        B, S, E = (2, 256, 512)
        H, KVH, D = (32, 8, 128)
        GROUPS = H // KVH
        MAX_POS = 512
        ROPE_THETA = 10000.0

        def _rope_tables(max_pos, dim, theta):
            inv_freq = 1.0 / theta ** (jnp.arange(0, dim, 2, dtype=jnp.float32) / dim)
            t = jnp.arange(max_pos, dtype=jnp.float32)
            freqs = jnp.einsum('i,j->ij', t, inv_freq)
            emb = jnp.concatenate([freqs, freqs], axis=-1)
            return (jnp.cos(emb), jnp.sin(emb))

        def _rotate_half(x):
            x1, x2 = (x[..., :x.shape[-1] // 2], x[..., x.shape[-1] // 2:])
            return jnp.concatenate([-x2, x1], axis=-1)
        key = jax.random.key(seed)
        ks = jax.random.split(key, 8)
        scale_w = 1.0 / np.sqrt(E)
        query = jax.random.normal(ks[0], (B, S, E), dtype=jnp.float32)
        k_in = jax.random.normal(ks[1], (B, S, E), dtype=jnp.float32)
        v_in = jax.random.normal(ks[2], (B, S, E), dtype=jnp.float32)
        position_ids = jnp.broadcast_to(jnp.arange(S, dtype=jnp.int64), (B, S))
        src_mask = jnp.tril(jnp.ones((S, S), dtype=jnp.int32))
        src_mask = jnp.broadcast_to(src_mask, (B, S, S))
        Wq = jax.random.normal(ks[3], (E, H * D), dtype=jnp.float32) * scale_w
        Wk = jax.random.normal(ks[4], (E, KVH * D), dtype=jnp.float32) * scale_w
        Wv = jax.random.normal(ks[5], (E, KVH * D), dtype=jnp.float32) * scale_w
        Wo = jax.random.normal(ks[6], (H * D, E), dtype=jnp.float32) * scale_w
        return {'query': query, 'key': k_in, 'value': v_in, 'position_ids': position_ids, 'src_mask': src_mask, 'Wq': Wq, 'Wk': Wk, 'Wv': Wv, 'Wo': Wo}
    _L0_xattn_all = _L0_xattn_setup()
    _L0_xattn_in = {k: v for k, v in _L0_xattn_all.items() if k in ('Wq', 'Wk', 'Wv', 'Wo')}
    del _L0_xattn_all

    def _L0_ffn_setup():
        import jax, jax.numpy as jnp
        import numpy as np

        @jax.custom_vjp
        def ste_sign(w):
            return jnp.sign(w)

        def _ste_fwd(w):
            return (jnp.sign(w), w)

        def _ste_bwd(w, g):
            mask = ((w > -1) & (w < 1)).astype(g.dtype)
            return (g * mask,)
        ste_sign.defvjp(_ste_fwd, _ste_bwd)
        key = jax.random.key(seed)
        k = jax.random.split(key, 6)
        B, S, H, O, E = (4, 256, 512, 512, 8)
        return {'x': jax.random.normal(k[0], (B, S, H), dtype=jnp.float32), 'weight': jax.random.normal(k[1], (O, H), dtype=jnp.float32) * 0.02, 'bias': jax.random.normal(k[2], (O,), dtype=jnp.float32) * 0.02, 'gate_w': jax.random.normal(k[3], (E, H), dtype=jnp.float32) * 0.02, 'in_channel_scale': jax.random.normal(k[4], (E, H), dtype=jnp.float32), 'out_channel_scale': jax.random.normal(k[5], (E, O), dtype=jnp.float32)}
    _L0_ffn_all = _L0_ffn_setup()
    _L0_ffn_in = {k: v for k, v in _L0_ffn_all.items() if k in ('weight', 'bias', 'gate_w', 'in_channel_scale', 'out_channel_scale')}
    del _L0_ffn_all
    return {'x': x, 'ctx_4096': ctx_4096, 'pos_BxS2': pos_BxS2, 'mask_BxSxS2_ik0': mask_BxSxS2_ik0, 'L0_xattn_Wq': _L0_xattn_in['Wq'], 'L0_xattn_Wk': _L0_xattn_in['Wk'], 'L0_xattn_Wv': _L0_xattn_in['Wv'], 'L0_xattn_Wo': _L0_xattn_in['Wo'], 'L0_ffn_weight': _L0_ffn_in['weight'], 'L0_ffn_bias': _L0_ffn_in['bias'], 'L0_ffn_gate_w': _L0_ffn_in['gate_w'], 'L0_ffn_in_channel_scale': _L0_ffn_in['in_channel_scale'], 'L0_ffn_out_channel_scale': _L0_ffn_in['out_channel_scale']}

def reference(x, ctx_4096, pos_BxS2, mask_BxSxS2_ik0, L0_xattn_Wq, L0_xattn_Wk, L0_xattn_Wv, L0_xattn_Wo, L0_ffn_weight, L0_ffn_bias, L0_ffn_gate_w, L0_ffn_in_channel_scale, L0_ffn_out_channel_scale):
    import jax
    import jax.numpy as jnp

    def _L0_xattn_ref(query, key, value, position_ids, src_mask, Wq, Wk, Wv, Wo):
        import jax, jax.numpy as jnp
        import numpy as np
        B, S, E = (2, 256, 512)
        H, KVH, D = (32, 8, 128)
        GROUPS = H // KVH
        MAX_POS = 512
        ROPE_THETA = 10000.0

        def _rope_tables(max_pos, dim, theta):
            inv_freq = 1.0 / theta ** (jnp.arange(0, dim, 2, dtype=jnp.float32) / dim)
            t = jnp.arange(max_pos, dtype=jnp.float32)
            freqs = jnp.einsum('i,j->ij', t, inv_freq)
            emb = jnp.concatenate([freqs, freqs], axis=-1)
            return (jnp.cos(emb), jnp.sin(emb))

        def _rotate_half(x):
            x1, x2 = (x[..., :x.shape[-1] // 2], x[..., x.shape[-1] // 2:])
            return jnp.concatenate([-x2, x1], axis=-1)
        nb, q_len, _ = query.shape
        q = (query @ Wq).reshape(nb, q_len, H, D).transpose(0, 2, 1, 3)
        k = (key @ Wk).reshape(nb, q_len, KVH, D).transpose(0, 2, 1, 3)
        v = (value @ Wv).reshape(nb, q_len, KVH, D).transpose(0, 2, 1, 3)
        cos_t, sin_t = _rope_tables(MAX_POS, D, ROPE_THETA)
        cos = cos_t[position_ids][:, None]
        sin = sin_t[position_ids][:, None]
        q = q * cos + _rotate_half(q) * sin
        k = k * cos + _rotate_half(k) * sin
        k = jnp.repeat(k, GROUPS, axis=1)
        v = jnp.repeat(v, GROUPS, axis=1)
        scores = jnp.einsum('bhqd,bhkd->bhqk', q, k) / jnp.sqrt(jnp.float32(D))
        mask = src_mask[:, None]
        scores = jnp.where(mask == 0, jnp.float32(-1000000000.0), scores)
        attn = jax.nn.softmax(scores, axis=-1)
        x = jnp.einsum('bhqk,bhkd->bhqd', attn, v)
        x = x.transpose(0, 2, 1, 3).reshape(nb, q_len, H * D)
        return x @ Wo

    def _L0_ffn_ref(x, weight, bias, gate_w, in_channel_scale, out_channel_scale):
        import jax, jax.numpy as jnp
        import numpy as np

        @jax.custom_vjp
        def ste_sign(w):
            return jnp.sign(w)

        def _ste_fwd(w):
            return (jnp.sign(w), w)

        def _ste_bwd(w, g):
            mask = ((w > -1) & (w < 1)).astype(g.dtype)
            return (g * mask,)
        ste_sign.defvjp(_ste_fwd, _ste_bwd)
        B, S, H = x.shape
        xf = x.reshape(-1, H)
        router_logits = xf @ gate_w.T
        routing = jax.nn.softmax(router_logits.astype(jnp.float32), axis=1).astype(x.dtype)
        in_scale = routing @ in_channel_scale
        out_scale = routing @ out_channel_scale
        wb = ste_sign(weight)
        out = xf * in_scale @ wb.T * out_scale + bias
        return out.reshape(B, S, -1)
    x = x + _L0_xattn_ref(_layernorm(x, axis=-1), ctx_4096, ctx_4096, pos_BxS2, mask_BxSxS2_ik0, L0_xattn_Wq, L0_xattn_Wk, L0_xattn_Wv, L0_xattn_Wo)
    x = x + _L0_ffn_ref(_layernorm(x, axis=-1), L0_ffn_weight, L0_ffn_bias, L0_ffn_gate_w, L0_ffn_in_channel_scale, L0_ffn_out_channel_scale)
    return x

_drawn_inputs = setup_inputs


def setup_inputs(seed=0):
    import zlib

    import numpy as np

    out = dict(_drawn_inputs(seed))
    spreads = {}
    factors = {'L0_ffn_bias': 8.0}
    for name, (base, spread) in spreads.items():
        noise = np.random.default_rng([zlib.crc32(name.encode()), seed]).standard_normal(out[name].shape)
        drawn = base * np.exp(spread * noise) if base else spread * noise
        out[name] = jnp.asarray(drawn.astype(out[name].dtype))
    for name, factor in factors.items():
        out[name] = (out[name] * factor).astype(out[name].dtype)
    return out
```

```python
import concourse.bass as bass
from concourse import mybir
from contextlib import ExitStack

F32 = mybir.dt.float32
F32R = mybir.dt.float32r
I32 = mybir.dt.int32
ALU = mybir.AluOpType
ACT = mybir.ActivationFunctionType
AX = mybir.AxisListType


def attention_ffn(nc, x, ctx_in, pos, mask, wq, wk, wv, wo, ffn_w, ffn_bias, gate_w, in_scale, out_scale,
                  rope, out):
    B, S, E = x.shape
    D = 128
    H, KVH = wq.shape[1] // D, wk.shape[1] // D
    HG = H // KVH
    NE = gate_w.shape[0]
    MAXPOS = rope.shape[0]
    P = 128
    EC = E // P
    HALVES = 2
    TILES = B * S // P // HALVES
    TOK = TILES * P
    BLOCKS = 2
    BT = TOK // BLOCKS
    PAIRS = BT // P
    SLOTS = KVH * BLOCKS
    KQ = 1 + HG
    PROJ = KQ + 1
    CH = PROJ + HG
    RING = 5
    SCALE = float(D) ** -0.5
    MASKED = -1.0e9 / SCALE
    EPS = 1e-5
    assert CH % RING == 0 and BT == 512 and 2 * S == P

    x_t = x.rearrange("(n b) s e -> n (b s) e", b=2)
    ctx_t = ctx_in.rearrange("(n b) s e -> n (b s) e", b=2)
    out_t = out.rearrange("(n b) s e -> n (b s) e", b=2)
    wq_c = wq.rearrange("(c p) n -> p c n", p=P)
    wk_c = wk.rearrange("(c p) n -> p c n", p=P)
    wv_c = wv.rearrange("(c p) n -> p c n", p=P)

    stack = ExitStack()
    with stack:
        def sb(name, shape, dt=F32):
            return stack.enter_context(nc.sbuf_tensor(name, shape, dt))

        def sem(name):
            return stack.enter_context(nc.semaphore(name))

        xT_hi, xT_lo = (sb(n, [P, EC, TOK], F32R) for n in ("xT_hi", "xT_lo"))
        cT_hi, cT_lo = (sb(n, [P, EC, TOK], F32R) for n in ("cT_hi", "cT_lo"))
        acc = sb("acc", [P, TILES, E])
        cosT, sinT = sb("cosT", [P, TOK]), sb("sinT", [P, TOK])
        w_hi, w_lo = (sb(n, [P, PROJ, EC, P], F32R) for n in ("w_hi", "w_lo"))
        wo_hi, wo_lo = (sb(n, [P, HG, E], F32R) for n in ("wo_hi", "wo_lo"))
        raw = sb("raw", [P, RING, E])
        qT = sb("qT", [P, HG // 2, 2 * BT])
        kT = sb("kT", [P, BT])
        vT = sb("vT", [P, BT])
        v = sb("v", [P, PAIRS, D])
        oT_hi, oT_lo = (sb(n, [P, PAIRS, HG, P], F32R) for n in ("oT_hi", "oT_lo"))
        scores = sb("scores", [P, TILES, 2 * P])
        msk = sb("msk", [P, TILES, P], I32)
        probs = sb("probs", [P, PAIRS, 2, 2, S])
        pT = sb("pT", [P, 2, 2, 2 * P])
        swp = sb("swp", [P, 2, BT])
        rot = sb("rot", [P, 2, BT])
        ident = sb("ident", [P, P])
        stats = sb("stats", [P, TILES, 6])
        mv = sb("mv", [P, TILES, 2])
        std = sb("std", [P, TILES])
        rstd = sb("rstd", [P, TILES])
        smax = sb("smax", [P, 2, 4])
        ssum = sb("ssum", [P, 2, 4])
        srec = sb("srec", [P, 2, 4])
        pos_i = sb("pos_i", [P, HALVES * TILES], I32)
        pos_f = sb("pos_f", [P, HALVES * TILES])
        pos_w = sb("pos_w", [P, HALVES * TILES])
        pos_u = sb("pos_u", [P, HALVES * TILES], I32)
        pos_use = sb("pos_use", [P, TILES], I32)
        eps = sb("eps", [P, 1])
        gateT = sb("gateT", [P, EC, NE])
        route = sb("route", [P, 2, P])
        routeT = sb("routeT", [P, 2, P])
        rexp = sb("rexp", [P, 2, NE])
        rmax, rsum, rrec = sb("rmax", [P, 2]), sb("rsum", [P, 2]), sb("rrec", [P, 2])

        rope_rows = scores
        tok4 = qT[:, :, :].rearrange("p a (b n) -> p (a b) n", n=E)
        sgnT = w_hi[:, 1:1 + EC, :, :].rearrange("p a c n -> p a (c n)")
        xs_hi = oT_hi[:, :, :, :].rearrange("p a h n -> p a (h n)")
        xs_lo = oT_lo[:, :, :, :].rearrange("p a h n -> p a (h n)")
        bias_b = kT
        in_sc, out_sc = vT, v[:, :, :].rearrange("p a n -> p (a n)")

        chunk = [stack.enter_context(nc.psum_tensor(f"chunk{i}", [P, 512], F32)) for i in range(3)]
        sc_ps = [stack.enter_context(nc.psum_tensor(f"sc_ps{i}", [P, 512], F32)) for i in range(2)]
        tr_ps = stack.enter_context(nc.psum_tensor("tr_ps", [P, 512], F32))
        o_ps = [stack.enter_context(nc.psum_tensor(f"o_ps{i}", [P, 512], F32)) for i in range(2)]

        half_open, waits_passed = sem("half_open"), sem("waits_passed")
        raw_in = [sem(f"raw_in{r}") for r in range(RING)]
        x_in = [sem(f"x_in{k}") for k in range(TILES // 2)]
        c_in = [sem(f"c_in{k}") for k in range(2)]
        mask_in, pos_in, gate_in = sem("mask_in"), sem("pos_in"), sem("gate_in")
        out_done = [sem(f"out_done{k}") for k in range(2)]
        ident_ok, zeros_ok = sem("ident_ok"), sem("zeros_ok")
        pos1, pos2, pos_ok = sem("pos1"), sem("pos2"), sem("pos_ok")
        rows_in = [sem(f"rows_in{i}") for i in range(TILES)]
        rows_tr, rope_ok = sem("rows_tr"), sem("rope_ok")
        fill_ok = sem("fill_ok")
        stat1, stat2, std_ok, rstd_ok = sem("stat1"), sem("stat2"), sem("std_ok"), sem("rstd_ok")
        xn_ok, x_tr, x_hi, x_lo = sem("xn_ok"), sem("x_tr"), sem("x_hi"), sem("x_lo")
        c_tr, c_hi, c_lo = sem("c_tr"), sem("c_hi"), sem("c_lo")
        wsplit_hi, wsplit_lo = sem("wsplit_hi"), sem("wsplit_lo")
        proj_done, outproj_done = sem("proj_done"), sem("outproj_done")
        swapped, cos_done, sin_done, roped = sem("swapped"), sem("cos_done"), sem("sin_done"), sem("roped")
        vT_ok, v_tr, v_ok = sem("vT_ok"), sem("v_tr"), sem("v_ok")
        scores_done, masked, maxed, shifted = sem("scores_done"), sem("masked"), sem("maxed"), sem("shifted")
        exped, summed, recd, probs_ok = sem("exped"), sem("summed"), sem("recd"), sem("probs_ok")
        probs_tr, pT_a, pT_b = sem("probs_tr"), sem("pT_a"), sem("pT_b")
        pv_done, o_hi, o_lo, added = sem("pv_done"), sem("o_hi"), sem("o_lo"), sem("added")
        gate_tr, gate_ok = sem("gate_tr"), sem("gate_ok")
        fw_in, fw_neg, fw_sgn, fw_tr, fw_ok = sem("fw_in"), sem("fw_neg"), sem("fw_sgn"), sem("fw_tr"), sem("fw_ok")
        sc_zero, sc_in = sem("sc_zero"), sem("sc_in")
        fn_ok, fn_tr, fn_T = sem("fn_ok"), sem("fn_tr"), sem("fn_T")
        lg_done, rm_ok, re_ok, rr_ok, rt_ok = sem("lg_done"), sem("rm_ok"), sem("re_ok"), sem("rr_ok"), sem("rt_ok")
        rt_tr, rtT_ok, isc_done, osc_done, osc_ok = (sem(n) for n in ("rt_tr", "rtT_ok", "isc_done", "osc_done", "osc_ok"))
        xs_ok, xs_h, xs_l, f_done, biased = (sem(n) for n in ("xs_ok", "xs_h", "xs_l", "f_done", "biased"))
        y_mul, y_ok = sem("y_mul"), sem("y_ok")

        OUT_BANK = [0, 1, 2, 0]
        PROJ_BANK = [1, 2, 0, 1, 2, 1]

        block = stack.enter_context(nc.Block())

        def slots_of_half(eng, th, slot):
            slot(th, 0, 0, False, False, True, 0)
            slot(th, 1, 1, False, True, True, 0)
            with eng.Fori(1, KVH) as g:
                slot(th, 2 * g, 0, True, True, True, g)
                slot(th, 2 * g + 1, 1, True, True, True, g)
            slot(th, SLOTS, 0, True, True, False, KVH)
            slot(th, SLOTS + 1, 1, True, False, False, KVH)

        def tiles_of_half(eng, th, step):
            for k in range(2):
                step(th * TILES + k, k, k, True)
            with eng.Fori(1, TILES // 2) as i:
                for k in range(2):
                    step(th * TILES + 2 * i + k, 2 * i + k, k, False)

        def one(tile):
            return slice(tile, tile + 1) if isinstance(tile, int) else bass.ds(tile, 1)

        def cols(tile):
            return slice(tile * P, tile * P + P) if isinstance(tile, int) else bass.ds(tile * P, P)

        def row(buffer, tile):
            return buffer[:, one(tile), :].rearrange("p a n -> p (a n)")

        def row_of(dram, t):
            return dram[bass.ds(t, 1)].rearrange("a p n -> (a p) n")

        def by_chunk(bank):
            return bank[:, :].rearrange("p (c n) -> p c n", n=P)

        def wait_alone(eng, semaphore, count):
            eng.wait_ge(semaphore, count)
            eng.sem_inc(waits_passed, 1)

        def U_of(th, u):
            return th * SLOTS + u

        @block.sync
        def _(sp):
            sp.dma_start(pos_i[:, :], pos.rearrange("(n b) s -> (b s) n", b=2),
                         allow_slow_non_contiguous=True).then_inc(pos_in, 16)
            sp.wait_ge(zeros_ok, 3)
            sp.dma_start(kT[0:NE, :], gate_w).then_inc(gate_in, 16)
            sp.wait_ge(gate_ok, 1)

            def load_group(th, g, first):
                for c in range(CH):
                    r = c % RING
                    if not (first and c < RING):
                        sp.wait_ge(wsplit_lo, (th * KVH + g) * CH + c - RING + 1)
                    if c < PROJ:
                        src = (wk_c[:, :, bass.ts(g, D)] if c == 0 else
                               wv_c[:, :, bass.ts(g, D)] if c == PROJ - 1 else
                               wq_c[:, :, bass.ts(g * HG + (c - 1), D)])
                        sp.dma_start(raw[:, r, :].rearrange("p (c n) -> p c n", n=P), src).then_inc(raw_in[r], 16)
                    else:
                        sp.dma_start(raw[:, r, :], wo[bass.ts(g * HG + (c - PROJ), D), :]).then_inc(raw_in[r], 16)

            with sp.Fori(0, HALVES) as th:
                sp.wait_ge(half_open, th + 1)
                for c in range(2):
                    sp.dma_start(msk[c * S:(c + 1) * S, :, :].rearrange("s n (b t) -> s n b t", b=2),
                                 mask.rearrange("(h n b) s t -> h s n b t", h=HALVES, b=2)[th]).then_inc(mask_in, 16)
                for i in range(TILES // 2):
                    sp.dma_start(acc[:, 2 * i:2 * i + 2, :],
                                 x_t[bass.ds(th * TILES + 2 * i, 2)].rearrange("a p n -> p a n")).then_inc(x_in[i], 16)

                def load(t, tile, k, first):
                    if not first:
                        sp.wait_ge(c_tr, t - 1)
                    sp.dma_start(tok4[:, k, :], row_of(ctx_t, t)).then_inc(c_in[k], 16)

                tiles_of_half(sp, th, load)
                load_group(th, 0, True)
                with sp.Fori(1, KVH) as g:
                    load_group(th, g, False)
                sp.wait_ge(wsplit_lo, (th + 1) * KVH * CH)
                sp.dma_start(raw[:, 0:EC, :], ffn_w.rearrange("(c p) n -> p c n", p=P)).then_inc(fw_in, 16)
                sp.wait_ge(sc_zero, 2 * (th + 1))
                sp.dma_start(in_sc[0:NE, :], in_scale).then_inc(sc_in, 16)
                sp.dma_start(out_sc[0:NE, :], out_scale).then_inc(sc_in, 16)
                sp.dma_start(bias_b[:, :], ffn_bias.rearrange("(a n) -> a n", a=1).to_broadcast([P, E])).then_inc(sc_in, 16)

                def store(t, tile, k, first):
                    sp.wait_ge(y_ok, t + 1)
                    sp.dma_start(row_of(out_t, t), raw[:, k, :]).then_inc(out_done[k], 16)

                tiles_of_half(sp, th, store)
                for k in range(2):
                    wait_alone(sp, out_done[k], 16 * TILES // 2 * (th + 1))

        @block.gpsimd
        def _(pool):
            nc.gpsimd.memset(ident[:, :], 0.0).then_inc(ident_ok, 1)
            pool.wait_ge(ident_ok, 1)
            nc.gpsimd.affine_select(out=ident[:, :], in_=ident[:, :], compare_op=ALU.not_equal, fill=1.0,
                                    base=0, pattern=[[-1, P]], channel_multiplier=1).then_inc(ident_ok, 1)
            nc.gpsimd.memset(kT[:, :], 0.0).then_inc(zeros_ok, 1)
            nc.gpsimd.memset(pT[:, :, :, :], 0.0).then_inc(zeros_ok, 1)
            nc.gpsimd.memset(route[:, :, :], 0.0).then_inc(zeros_ok, 1)

            def split_lo(th, g, c):
                n = (th * KVH + g) * CH + c
                pool.wait_ge(wsplit_hi, n + 1)
                if c < PROJ:
                    hi = w_hi[:, c, :, :].rearrange("p c n -> p (c n)")
                    lo = w_lo[:, c, :, :].rearrange("p c n -> p (c n)")
                else:
                    hi, lo = wo_hi[:, c - PROJ, :], wo_lo[:, c - PROJ, :]
                nc.gpsimd.tensor_tensor(lo, raw[:, c % RING, :], hi.bitcast(F32), ALU.subtract).then_inc(wsplit_lo, 1)

            def slot(th, u, tb, wo_, attn, proj, g):
                if not proj:
                    return
                if tb == 0:
                    for c in range(PROJ):
                        split_lo(th, g, c)
                else:
                    for c in range(PROJ, CH):
                        split_lo(th, g, c)

            with pool.Fori(0, HALVES) as th:
                pool.wait_ge(half_open, th + 1)
                wait_alone(pool, pos_ok, th + 1)
                for i in range(TILES):
                    nc.gpsimd.indirect_dma_start(
                        rope_rows[:, i, :], None, rope,
                        bass.IndirectOffsetOnAxis(ap=pos_use[:, i:i + 1], axis=0)).then_inc(rows_in[i], 16)
                wait_alone(pool, rows_tr, (th + 1) * TILES)
                nc.gpsimd.memset(scores[:, :, :], MASKED).then_inc(fill_ok, 1)
                slots_of_half(pool, th, slot)
                wait_alone(pool, pv_done, (th + 1) * SLOTS * PAIRS)
                nc.gpsimd.memset(in_sc[:, :], 0.0).then_inc(sc_zero, 1)
                nc.gpsimd.memset(out_sc, 0.0).then_inc(sc_zero, 1)
                pool.wait_ge(sc_in, 48 * (th + 1))

                def add_bias(t, tile, k, first):
                    pool.wait_ge(fn_ok, t + 1)
                    nc.gpsimd.tensor_tensor(row(acc, tile), row(acc, tile), bias_b[:, :], ALU.add).then_inc(biased, 1)

                tiles_of_half(pool, th, add_bias)

        @block.scalar
        def _(act):
            def copy(dst, src):
                return nc.scalar.activation(dst, src, ACT.Copy)

            def split_hi(th, g, c, reuse):
                IT = th * KVH + g
                act.wait_ge(raw_in[c % RING], 16 * (IT * (CH // RING) + c // RING + 1))
                if c < PROJ:
                    if reuse:
                        act.wait_ge(proj_done, (2 * IT - 1) * PROJ + c + 1)
                    hi = w_hi[:, c, :, :].rearrange("p c n -> p (c n)")
                else:
                    if reuse:
                        act.wait_ge(outproj_done, 2 * IT * PAIRS)
                    hi = wo_hi[:, c - PROJ, :]
                copy(hi, raw[:, c % RING, :]).then_inc(wsplit_hi, 1)

            def slot(th, u, tb, wo_, attn, proj, g):
                U = U_of(th, u)
                first = isinstance(u, int) and u == 1
                peeled = isinstance(u, int) and u < BLOCKS

                def hi_chunk(c):
                    if proj:
                        split_hi(th, g, c, not peeled)

                def exp_pair(p):
                    act.wait_ge(shifted, (U - 1) * PAIRS + p + 1)
                    s = probs[:, p, :, :, :].rearrange("p a b t -> p (a b t)")
                    nc.scalar.activation(s, s, ACT.Exp, scale=SCALE).then_inc(exped, 1)

                def pT_first(p):
                    act.wait_ge(probs_tr, (U - 1) * PAIRS + p + 1)
                    if not (first and p < 2):
                        act.wait_ge(pv_done, (U - 1) * PAIRS + p - 1)
                    copy(pT[0:S, p % 2, 0, :], tr_ps[0:S, 0:2 * P]).then_inc(pT_a, 1)

                def out_hi(p):
                    act.wait_ge(pv_done, (U - 1) * PAIRS + p + 1)
                    if not first:
                        act.wait_ge(outproj_done, (U - 2) * PAIRS + p + 1)
                    copy(oT_hi[:, p, :, :].rearrange("p h (b s) -> p b h s", b=2),
                         o_ps[p % 2][:, :].rearrange("p (b h s) -> p b h s", b=2, h=HG)).then_inc(o_hi, 1)

                def swap(j):
                    if not proj:
                        return
                    bank = chunk[PROJ_BANK[j]]
                    act.wait_ge(proj_done, U * PROJ + j + 1)
                    if not (peeled and u == 0 and j < 2):
                        act.wait_ge(roped, U * KQ + j - 1)
                    s = swp[:, (tb + j) % 2, :]
                    copy(s[0:D // 2, :], bank[D // 2:D, :])
                    copy(s[D // 2:D, :], bank[0:D // 2, :]).then_inc(swapped, 1)

                if attn:
                    act.wait_ge(v_tr, U)
                    if not first:
                        act.wait_ge(pv_done, (U - 1) * PAIRS)
                    copy(v[:, :, :].rearrange("p a n -> p (a n)"), tr_ps[:, :]).then_inc(v_ok, 1)
                if tb == 0:
                    hi_chunk(0)
                    if attn:
                        exp_pair(0)
                    hi_chunk(1)
                    if attn:
                        exp_pair(1)
                    hi_chunk(2)
                    if attn:
                        pT_first(0)
                        exp_pair(2)
                    hi_chunk(3)
                    if attn:
                        pT_first(1)
                        out_hi(0)
                        exp_pair(3)
                    hi_chunk(4)
                    hi_chunk(5)
                elif attn:
                    exp_pair(0)
                    exp_pair(1)
                    pT_first(0)
                    exp_pair(2)
                    pT_first(1)
                    out_hi(0)
                    exp_pair(3)
                swap(0)
                if attn:
                    pT_first(2)
                    out_hi(1)
                if tb == 1:
                    hi_chunk(6)
                swap(1)
                if attn:
                    pT_first(3)
                    out_hi(2)
                if tb == 1:
                    hi_chunk(7)
                swap(2)
                if attn:
                    out_hi(3)
                if tb == 1:
                    hi_chunk(8)
                swap(3)
                if tb == 1:
                    hi_chunk(9)
                swap(4)
                if proj:
                    act.wait_ge(proj_done, (U + 1) * PROJ)
                    if not (peeled and u == 0):
                        act.wait_ge(v_tr, U)
                    copy(vT[:, :], chunk[PROJ_BANK[PROJ - 1]][:, :]).then_inc(vT_ok, 1)

            act.wait_ge(gate_tr, 1)
            copy(gateT[:, :, :], chunk[0][:, :].rearrange("p (c n) -> p c n", n=P)[:, :, 0:NE]).then_inc(gate_ok, 1)

            with act.Fori(0, HALVES) as th:
                act.wait_ge(half_open, th + 1)
                act.wait_ge(stat2, (th + 1) * (2 * TILES) - TILES)
                nc.scalar.activation(std[:, :], mv[:, :, 1], ACT.Sqrt, bias=eps[:, :]).then_inc(std_ok, 1)
                for i in range(TILES):
                    act.wait_ge(rows_tr, th * TILES + i + 1)
                    copy(cosT[:, bass.ts(i, P)], sc_ps[i % 2][:, 0:P])
                    copy(sinT[:, bass.ts(i, P)], sc_ps[i % 2][:, P:2 * P]).then_inc(rope_ok, 1)

                def tile_hi(t, tile, k, first):
                    act.wait_ge(c_tr, t + 1)
                    copy(cT_hi[:, :, cols(tile)], by_chunk(o_ps[k])).then_inc(c_hi, 1)
                    act.wait_ge(x_tr, t + 1)
                    copy(xT_hi[:, :, cols(tile)], by_chunk(chunk[k])).then_inc(x_hi, 1)

                tiles_of_half(act, th, tile_hi)
                slots_of_half(act, th, slot)

                act.wait_ge(stat2, (th + 1) * (2 * TILES))
                nc.scalar.activation(std[:, :], mv[:, :, 1], ACT.Sqrt, bias=eps[:, :]).then_inc(std_ok, 1)
                for c in range(EC):
                    act.wait_ge(fw_tr, th * EC + c + 1)
                    copy(sgnT[:, c, :], sc_ps[c % 2][:, :]).then_inc(fw_ok, 1)


                def ffn_tile(t, tile, k, first):
                    act.wait_ge(fn_tr, t + 1)
                    if not first:
                        act.wait_ge(lg_done, t - 1)
                        act.wait_ge(xs_ok, t - 1)
                    copy(tok4[:, 2 + k, :], chunk[k][:, :]).then_inc(fn_T, 1)
                    act.wait_ge(rm_ok, t + 1)
                    if not first:
                        act.wait_ge(rt_ok, t - 1)
                    nc.scalar.activation(rexp[:, k, :], tr_ps[:, 0:NE], ACT.Exp, bias=rmax[:, k:k + 1],
                                         accum_out=rsum[:, k:k + 1]).then_inc(re_ok, 1)
                    act.wait_ge(rt_tr, t + 1)
                    if not first:
                        act.wait_ge(osc_done, t - 1)
                    copy(routeT[:, k, :], tr_ps[:, 0:P]).then_inc(rtT_ok, 1)
                    act.wait_ge(osc_done, t + 1)
                    if not first:
                        act.wait_ge(y_mul, t - 1)
                    copy(swp[:, k, :], sc_ps[k][:, :]).then_inc(osc_ok, 1)
                    act.wait_ge(xs_ok, t + 1)
                    if not first:
                        act.wait_ge(f_done, t - 1)
                    copy(xs_hi[:, k, :], rot[:, k, :]).then_inc(xs_h, 1)

                tiles_of_half(act, th, ffn_tile)

        @block.vector
        def _(dve):
            def lo_of(dst, src, hi):
                return nc.vector.tensor_tensor(dst, src, hi.bitcast(F32), ALU.subtract)

            def norm_stats(n0, src_ready):
                for i in range(TILES):
                    src_ready(i)
                    nc.vector.bn_stats(stats[:, i, :], acc[:, i, :]).then_inc(stat1, 1)
                    wait_alone(dve, stat1, n0 + i + 1)
                    nc.vector.bn_aggr(mv[:, i, :], stats[:, i, :]).then_inc(stat2, 1)

            def slot(th, u, tb, wo_, attn, proj, g):
                U = U_of(th, u)
                first = isinstance(u, int) and u == 1
                peeled = isinstance(u, int) and u < BLOCKS

                def add_out(p):
                    if not wo_:
                        return
                    dve.wait_ge(outproj_done, (U - 2) * PAIRS + p + 1)
                    a = acc[:, tb * PAIRS + p, :]
                    nc.vector.tensor_tensor(a, chunk[OUT_BANK[p]][:, :], a, ALU.add).then_inc(added, 1)

                def soft_a(p):
                    if not attn:
                        return
                    n = (U - 1) * PAIRS + p
                    tile = (1 - tb) * PAIRS + p
                    sc4 = scores[:, tile, :].rearrange("p (a b t) -> p a b t", a=2, b=2)
                    wait_alone(dve, scores_done, n + 1)
                    nc.vector.copy_predicated(
                        scores[:, tile, :].rearrange("p (a n) -> p a n", a=2),
                        msk[:, tile, :].unsqueeze(1).to_broadcast([P, 2, P]),
                        sc_ps[p % 2][:, 0:2 * P].rearrange("p (a n) -> p a n", a=2)).then_inc(masked, 1)
                    dve.wait_ge(masked, n + 1)
                    mx = smax[:, p % 2, :]
                    nc.vector.tensor_reduce(mx, scores[:, tile, :].rearrange("p (a t) -> p a t", t=S), AX.X, ALU.max).then_inc(maxed, 1)
                    dve.wait_ge(maxed, n + 1)
                    if not first:
                        dve.wait_ge(probs_tr, (U - 2) * PAIRS + p + 1)
                    nc.vector.tensor_tensor(
                        probs[:, p, :, :, :].rearrange("p a b t -> p (a b) t"),
                        scores[:, tile, :].rearrange("p (a t) -> p a t", t=S),
                        mx.unsqueeze(2).to_broadcast([P, 4, S]), ALU.subtract).then_inc(shifted, 1)

                def soft_b(p):
                    if not attn:
                        return
                    n = (U - 1) * PAIRS + p
                    e = probs[:, p, :, :, :].rearrange("p a b t -> p (a b) t")
                    dve.wait_ge(exped, n + 1)
                    nc.vector.tensor_reduce(ssum[:, p % 2, :], e, AX.X, ALU.add).then_inc(summed, 1)
                    dve.wait_ge(summed, n + 1)
                    nc.vector.reciprocal(srec[:, p % 2, :], ssum[:, p % 2, :]).then_inc(recd, 1)
                    dve.wait_ge(recd, n + 1)
                    nc.vector.tensor_tensor(e, e, srec[:, p % 2, :].unsqueeze(2).to_broadcast([P, 4, S]),
                                            ALU.mult).then_inc(probs_ok, 1)

                def pT_second(p):
                    if not attn:
                        return
                    dve.wait_ge(probs_tr, (U - 1) * PAIRS + p + 1)
                    if not (first and p < 2):
                        dve.wait_ge(pv_done, (U - 1) * PAIRS + p - 1)
                    nc.vector.tensor_copy(pT[S:P, p % 2, 1, :], tr_ps[S:P, 0:2 * P]).then_inc(pT_b, 1)

                def out_lo(p):
                    if not attn:
                        return
                    dve.wait_ge(o_hi, (U - 1) * PAIRS + p + 1)
                    lo_of(oT_lo[:, p, :, :].rearrange("p h (b s) -> p b h s", b=2),
                          o_ps[p % 2][:, :].rearrange("p (b h s) -> p b h s", b=2, h=HG),
                          oT_hi[:, p, :, :].rearrange("p h (b s) -> p b h s", b=2)).then_inc(o_lo, 1)

                def rotate(j):
                    if not proj:
                        return
                    n = U * KQ + j
                    k = (tb + j) % 2
                    dve.wait_ge(swapped, n + 1)
                    nc.vector.tensor_tensor(rot[:, k, :], chunk[PROJ_BANK[j]][:, :], cosT[:, bass.ts(tb, BT)], ALU.mult).then_inc(cos_done, 1)
                    nc.vector.tensor_tensor(swp[:, k, :], swp[:, k, :], sinT[:, bass.ts(tb, BT)], ALU.mult).then_inc(sin_done, 1)
                    dve.wait_ge(cos_done, n + 1)
                    dve.wait_ge(sin_done, n + 1)
                    if attn and j == 0:
                        dve.wait_ge(scores_done, U * PAIRS)
                    if j == 0:
                        dst, r, s = kT[:, :], rot[:, k, :], swp[:, k, :]
                    else:
                        h = j - 1
                        dst = qT[:, h // 2, :].rearrange("p (b a s) -> p b a s", a=2, s=S)[:, :, h % 2, :]
                        r = rot[:, k, :].rearrange("p (b s) -> p b s", s=S)
                        s = swp[:, k, :].rearrange("p (b s) -> p b s", s=S)
                    nc.vector.tensor_tensor(dst, r, s, ALU.add).then_inc(roped, 1)

                add_out(0)
                soft_a(0)
                add_out(1)
                soft_b(0)
                soft_a(1)
                add_out(2)
                soft_b(1)
                soft_a(2)
                pT_second(0)
                add_out(3)
                soft_b(2)
                soft_a(3)
                pT_second(1)
                soft_b(3)
                out_lo(0)
                pT_second(2)
                rotate(0)
                out_lo(1)
                pT_second(3)
                rotate(1)
                out_lo(2)
                rotate(2)
                out_lo(3)
                rotate(3)
                rotate(4)

            dve.wait_ge(zeros_ok, 3)
            dve.wait_ge(pos_in, 16)
            nc.vector.tensor_copy(pos_f[:, :], pos_i[:, :]).then_inc(pos1, 1)
            dve.wait_ge(pos1, 1)
            nc.vector.tensor_scalar(pos_w[:, :], pos_f[:, :], 0.0, float(MAXPOS), ALU.is_lt, ALU.mult).then_inc(pos2, 1)
            dve.wait_ge(pos2, 1)
            nc.vector.tensor_tensor(pos_f[:, :], pos_f[:, :], pos_w[:, :], ALU.add).then_inc(pos1, 1)
            dve.wait_ge(pos1, 2)
            nc.vector.tensor_scalar(pos_u[:, :], pos_f[:, :], 0.0, float(MAXPOS - 1), ALU.max, ALU.min).then_inc(pos2, 1)
            dve.wait_ge(pos2, 2)
            nc.vector.memset(eps[:, :], EPS).then_inc(half_open, 1)

            with dve.Fori(0, HALVES) as th:
                dve.wait_ge(half_open, th + 1)
                nc.vector.tensor_copy(pos_use[:, :], pos_u[:, bass.ds(th * TILES, TILES)]).then_inc(pos_ok, 1)
                norm_stats(th * 2 * TILES, lambda i: dve.wait_ge(x_in[i // 2], 16 * (th + 1)))
                dve.wait_ge(std_ok, 2 * th + 1)
                nc.vector.reciprocal(rstd[:, :], std[:, :]).then_inc(rstd_ok, 1)
                dve.wait_ge(rstd_ok, 2 * th + 1)

                def tile_in(t, tile, k, first):
                    if not first:
                        dve.wait_ge(x_tr, t - 1)
                    nc.vector.tensor_scalar(tok4[:, 2 + k, :], row(acc, tile), mv[:, one(tile), 0], rstd[:, one(tile)],
                                            ALU.subtract, ALU.mult).then_inc(xn_ok, 1)
                    dve.wait_ge(c_hi, t + 1)
                    lo_of(cT_lo[:, :, cols(tile)], by_chunk(o_ps[k]), cT_hi[:, :, cols(tile)]).then_inc(c_lo, 1)
                    dve.wait_ge(x_hi, t + 1)
                    lo_of(xT_lo[:, :, cols(tile)], by_chunk(chunk[k]), xT_hi[:, :, cols(tile)]).then_inc(x_lo, 1)

                tiles_of_half(dve, th, tile_in)
                dve.wait_ge(rope_ok, (th + 1) * TILES)
                dve.wait_ge(fill_ok, th + 1)
                dve.wait_ge(mask_in, 32 * (th + 1))
                slots_of_half(dve, th, slot)

                dve.wait_ge(fw_in, 16 * (th + 1))
                for c in range(EC):
                    nc.vector.tensor_scalar(rot[:, c % 2, :], raw[:, c, :], 0.0, None, ALU.is_lt).then_inc(fw_neg, 1)
                    dve.wait_ge(fw_neg, th * EC + c + 1)
                    nc.vector.scalar_tensor_tensor(raw[:, c, :], raw[:, c, :], 0.0, rot[:, c % 2, :],
                                                   ALU.is_gt, ALU.subtract).then_inc(fw_sgn, 1)
                dve.wait_ge(added, (th + 1) * SLOTS * PAIRS)
                norm_stats(th * 2 * TILES + TILES, lambda i: None)
                dve.wait_ge(std_ok, 2 * th + 2)
                nc.vector.reciprocal(rstd[:, :], std[:, :]).then_inc(rstd_ok, 1)
                dve.wait_ge(rstd_ok, 2 * th + 2)


                def ffn_tile(t, tile, k, first):
                    if not first:
                        dve.wait_ge(fn_tr, t - 1)
                    nc.vector.tensor_scalar(tok4[:, k, :], row(acc, tile), mv[:, one(tile), 0], rstd[:, one(tile)],
                                            ALU.subtract, ALU.mult).then_inc(fn_ok, 1)
                    dve.wait_ge(lg_done, t + 1)
                    nc.vector.tensor_reduce(rmax[:, k:k + 1], tr_ps[:, 0:NE], AX.X, ALU.max, negate=True).then_inc(rm_ok, 1)
                    dve.wait_ge(re_ok, t + 1)
                    nc.vector.reciprocal(rrec[:, k:k + 1], rsum[:, k:k + 1]).then_inc(rr_ok, 1)
                    dve.wait_ge(rr_ok, t + 1)
                    if not first:
                        dve.wait_ge(rt_tr, t - 1)
                    nc.vector.tensor_scalar(route[:, k, 0:NE], rexp[:, k, :], rrec[:, k:k + 1], None, ALU.mult).then_inc(rt_ok, 1)
                    dve.wait_ge(isc_done, t + 1)
                    dve.wait_ge(fn_T, t + 1)
                    nc.vector.tensor_tensor(rot[:, k, :], chunk[2][:, :], tok4[:, 2 + k, :], ALU.mult).then_inc(xs_ok, 1)
                    dve.wait_ge(xs_ok, t + 1)
                    dve.wait_ge(xs_h, t + 1)
                    if not first:
                        dve.wait_ge(f_done, t - 1)
                    lo_of(xs_lo[:, k, :], rot[:, k, :], xs_hi[:, k, :]).then_inc(xs_l, 1)
                    dve.wait_ge(f_done, t + 1)
                    dve.wait_ge(osc_ok, t + 1)
                    if not first:
                        dve.wait_ge(out_done[k], 8 * (t - k))
                    nc.vector.tensor_tensor(raw[:, k, :], o_ps[k][:, :], swp[:, k, :], ALU.mult).then_inc(y_mul, 1)
                    dve.wait_ge(y_mul, t + 1)
                    dve.wait_ge(biased, t + 1)
                    nc.vector.tensor_tensor(raw[:, k, :], raw[:, k, :], row(acc, tile), ALU.add).then_inc(y_ok, 1)

                tiles_of_half(dve, th, ffn_tile)
                dve.wait_ge(y_ok, (th + 1) * TILES)
                nc.vector.memset(eps[:, :], EPS).then_inc(half_open, 1)

        @block.tensor
        def _(pe):
            def transpose(dst, src):
                return nc.tensor.transpose(dst, src, ident[:, :])

            def split_products(bank, operands):
                last, n = None, len(operands)
                for i, (a_hi, a_lo, b_hi, b_lo) in enumerate(operands):
                    nc.tensor.matmul(bank, a_hi, b_hi, start=i == 0, stop=False)
                    nc.tensor.matmul(bank, a_hi, b_lo, start=False, stop=False)
                    last = nc.tensor.matmul(bank, a_lo, b_hi, start=False, stop=i == n - 1)
                return last

            def slot(th, u, tb, wo_, attn, proj, g):
                U = U_of(th, u)
                first = isinstance(u, int) and u == 1
                start = isinstance(u, int) and u == 0
                drained = isinstance(u, int) and u == SLOTS + 1

                def out_proj(p):
                    if not wo_:
                        return
                    n = (U - 2) * PAIRS + p
                    if p == 3:
                        pe.wait_ge(added, n - 2)
                    elif drained:
                        pe.wait_ge(added, (U - 3) * PAIRS + (4 if p == 0 else p + 1))
                    elif p == 0:
                        pe.wait_ge(cos_done, (U - 1) * KQ + 3)
                    elif p == 1:
                        pe.wait_ge(vT_ok, U)
                    else:
                        pe.wait_ge(cos_done, (U - 1) * KQ + 5)
                    pe.wait_ge(o_lo, n + 1)
                    ops = []
                    if tb == 0 and p == 0:
                        pe.wait_ge(wsplit_lo, (th * KVH + g) * CH)
                    for h in range(HG):
                        ops.append((oT_hi[:, p, h, :], oT_lo[:, p, h, :], wo_hi[:, h, :], wo_lo[:, h, :]))
                    split_products(chunk[OUT_BANK[p]][:, :], ops).then_inc(outproj_done, 1)

                def v_rows():
                    if not attn:
                        return
                    pe.wait_ge(vT_ok, U)
                    if not first:
                        pe.wait_ge(pT_a, (U - 1) * PAIRS)
                        pe.wait_ge(pT_b, (U - 1) * PAIRS)
                    for p in range(PAIRS):
                        last = transpose(tr_ps[:, p * D:(p + 1) * D], vT[:, p * P:(p + 1) * P])
                    last.then_inc(v_tr, 1)

                def scores_of(p):
                    if not attn:
                        return
                    n = (U - 1) * PAIRS + p
                    pe.wait_ge(roped, U * KQ)
                    if not (first and p < 2):
                        pe.wait_ge(masked, n - 1)
                    for hp in range(HG // 2):
                        for b in range(2):
                            bb = 2 * p + b
                            last = nc.tensor.matmul(sc_ps[p % 2][:, (2 * hp + b) * S:(2 * hp + b + 1) * S],
                                                    qT[:, hp, bb * P:(bb + 1) * P], kT[:, bb * S:(bb + 1) * S],
                                                    start=True, stop=True)
                    last.then_inc(scores_done, 1)

                def probs_T(p):
                    if not attn:
                        return
                    n = (U - 1) * PAIRS + p
                    pe.wait_ge(probs_ok, n + 1)
                    if p == 0:
                        pe.wait_ge(v_ok, U)
                    else:
                        pe.wait_ge(pT_a, n)
                        pe.wait_ge(pT_b, n)
                    for hp in range(2):
                        last = transpose(tr_ps[:, hp * P:(hp + 1) * P],
                                         probs[:, p, hp, :, :].rearrange("p b t -> p (b t)"))
                    last.then_inc(probs_tr, 1)

                def values(p):
                    if not attn:
                        return
                    n = (U - 1) * PAIRS + p
                    pe.wait_ge(pT_a, n + 1)
                    pe.wait_ge(pT_b, n + 1)
                    if not (first and p < 2):
                        pe.wait_ge(o_lo, n - 1)
                    nc.tensor.matmul(o_ps[p % 2][:, :], v[:, p, :], pT[:, p % 2, :, :].rearrange("p b n -> p (b n)"),
                                     start=True, stop=True).then_inc(pv_done, 1)

                def project(j):
                    if not proj:
                        return
                    if j == 0 and wo_:
                        pe.wait_ge(added, (U - 2) * PAIRS + 2)
                    elif j == 0 and not start:
                        pe.wait_ge(vT_ok, U)
                    elif j == 1 and wo_:
                        pe.wait_ge(added, (U - 2) * PAIRS + 3)
                    elif j == 1 and not start:
                        pe.wait_ge(cos_done, U * KQ)
                    elif j == 2 and wo_:
                        pe.wait_ge(added, (U - 2) * PAIRS + 4)
                    elif j == 2 and not start:
                        pe.wait_ge(cos_done, (U - 1) * KQ + 3)
                    elif j >= 3:
                        pe.wait_ge(cos_done, U * KQ + [1, 2, 4][j - 3])
                    if tb == 0:
                        pe.wait_ge(wsplit_lo, (th * KVH + g) * CH + j + 1)
                    src_hi, src_lo = (xT_hi, xT_lo) if 0 < j < PROJ - 1 else (cT_hi, cT_lo)
                    ops = [(w_hi[:, j, c, :], w_lo[:, j, c, :], src_hi[:, c, bass.ts(tb, BT)], src_lo[:, c, bass.ts(tb, BT)])
                           for c in range(EC)]
                    split_products(chunk[PROJ_BANK[j]][:, :], ops).then_inc(proj_done, 1)

                out_proj(0)
                v_rows()
                scores_of(0)
                out_proj(1)
                scores_of(1)
                out_proj(2)
                scores_of(2)
                probs_T(0)
                out_proj(3)
                scores_of(3)
                probs_T(1)
                values(0)
                project(0)
                probs_T(2)
                values(1)
                project(1)
                probs_T(3)
                values(2)
                project(2)
                values(3)
                project(3)
                project(4)
                project(5)

            pe.wait_ge(ident_ok, 2)
            pe.wait_ge(gate_in, 16)
            for c in range(EC):
                last = transpose(chunk[0][:, bass.ts(c, P)], kT[:, bass.ts(c, P)])
            last.then_inc(gate_tr, 1)
            pe.wait_ge(gate_ok, 1)

            with pe.Fori(0, HALVES) as th:
                pe.wait_ge(half_open, th + 1)
                for i in range(TILES):
                    pe.wait_ge(rows_in[i], 16 * (th + 1))
                    if i >= 2:
                        pe.wait_ge(rope_ok, th * TILES + i - 1)
                    transpose(sc_ps[i % 2][:, 0:P], rope_rows[:, i, 0:P])
                    transpose(sc_ps[i % 2][:, P:2 * P], rope_rows[:, i, P:2 * P]).then_inc(rows_tr, 1)

                def tile_T(t, tile, k, first):
                    if not first:
                        pe.wait_ge(c_lo, t - 1)
                    pe.wait_ge(c_in[k], 8 * (t - k) + 16)
                    for c in range(EC):
                        last = transpose(o_ps[k][:, bass.ts(c, P)], tok4[:, k, bass.ts(c, P)])
                    last.then_inc(c_tr, 1)
                    if not first:
                        pe.wait_ge(x_lo, t - 1)
                    pe.wait_ge(xn_ok, t + 1)
                    for c in range(EC):
                        last = transpose(chunk[k][:, bass.ts(c, P)], tok4[:, 2 + k, bass.ts(c, P)])
                    last.then_inc(x_tr, 1)

                tiles_of_half(pe, th, tile_T)
                pe.wait_ge(rope_ok, (th + 1) * TILES)
                pe.wait_ge(c_lo, (th + 1) * TILES)
                pe.wait_ge(x_lo, (th + 1) * TILES)
                slots_of_half(pe, th, slot)

                pe.wait_ge(fw_sgn, (th + 1) * EC)
                for c in range(EC):
                    if c >= 2:
                        pe.wait_ge(fw_ok, th * EC + c - 1)
                    for o in range(EC):
                        last = transpose(sc_ps[c % 2][:, bass.ts(o, P)], raw[:, o, bass.ts(c, P)])
                    last.then_inc(fw_tr, 1)
                pe.wait_ge(fw_ok, (th + 1) * EC)
                pe.wait_ge(sc_in, 48 * (th + 1))

                def ffn_tile(t, tile, k, first):
                    pe.wait_ge(fn_ok, t + 1)
                    if not first:
                        pe.wait_ge(fn_T, t - 1)
                    for c in range(EC):
                        last = transpose(chunk[k][:, bass.ts(c, P)], tok4[:, k, bass.ts(c, P)])
                    last.then_inc(fn_tr, 1)
                    pe.wait_ge(fn_T, t + 1)
                    if not (first and k == 0):
                        pe.wait_ge(rtT_ok, t)
                    for c in range(EC):
                        last = nc.tensor.matmul(tr_ps[:, 0:NE], tok4[:, 2 + k, bass.ts(c, P)], gateT[:, c, :],
                                                start=c == 0, stop=c == EC - 1)
                    last.then_inc(lg_done, 1)
                    pe.wait_ge(rt_ok, t + 1)
                    transpose(tr_ps[:, 0:P], route[:, k, :]).then_inc(rt_tr, 1)
                    pe.wait_ge(rtT_ok, t + 1)
                    if not (first and k == 0):
                        pe.wait_ge(xs_ok, t)
                    for c in range(EC):
                        last = nc.tensor.matmul(chunk[2][:, bass.ts(c, P)], in_sc[:, bass.ts(c, P)], routeT[:, k, :],
                                                start=True, stop=True)
                    last.then_inc(isc_done, 1)
                    if not first:
                        pe.wait_ge(osc_ok, t - 1)
                    nc.tensor.matmul(sc_ps[k][:, :], routeT[:, k, :], out_sc, start=True, stop=True).then_inc(osc_done, 1)
                    pe.wait_ge(xs_l, t + 1)
                    if not first:
                        pe.wait_ge(y_mul, t - 1)
                    for c in range(EC):
                        nc.tensor.matmul(o_ps[k][:, :], xs_hi[:, k, bass.ts(c, P)], sgnT[:, c, :], start=c == 0, stop=False)
                        last = nc.tensor.matmul(o_ps[k][:, :], xs_lo[:, k, bass.ts(c, P)], sgnT[:, c, :],
                                                start=False, stop=c == EC - 1)
                    last.then_inc(f_done, 1)

                tiles_of_half(pe, th, ffn_tile)


_INS = ["x", "ctx_4096", "pos_BxS2", "mask_BxSxS2_ik0", "L0_xattn_Wq", "L0_xattn_Wk", "L0_xattn_Wv", "L0_xattn_Wo",
        "L0_ffn_weight", "L0_ffn_bias", "L0_ffn_gate_w", "L0_ffn_in_channel_scale", "L0_ffn_out_channel_scale"]


def rope_table(positions=512, dim=128, theta=10000.0):
    import numpy as np
    inv = (1.0 / np.float32(theta) ** (np.arange(0, dim, 2, dtype=np.float32) / np.float32(dim))).astype(np.float32)
    angle = np.arange(positions, dtype=np.float32)[:, None] * inv[None, :]
    c, s = np.cos(angle), np.sin(angle)
    return np.concatenate([c, c, -s, s], axis=1).astype(np.float32)


def kernel(**inputs):
    import numpy as np
    import concourse.bacc as bacc
    from concourse.bass_utils import run_bass_kernel_spmd as run

    nc = bacc.Bacc("TRN2", target_bir_lowering=False, num_devices=1)
    arrays = {f"in_{n}": np.ascontiguousarray(inputs[n]) for n in _INS}
    arrays["rope_table"] = rope_table()
    args = [nc.dram_tensor(n, a.shape, mybir.dt.from_np(a.dtype), kind="ExternalInput").ap() for n, a in arrays.items()]
    shape = arrays["in_x"].shape
    args.append(nc.dram_tensor("result", shape, F32, kind="ExternalOutput").ap())
    attention_ffn(nc, *args)
    r = run(nc, [arrays], core_ids=[0])
    return r.results[0]["result"]
```

```python
import concourse.bass as bass
from concourse import mybir
from contextlib import ExitStack

F32 = mybir.dt.float32
F32R = mybir.dt.float32r
I32 = mybir.dt.int32
ALU = mybir.AluOpType
ACT = mybir.ActivationFunctionType
AX = mybir.AxisListType


def attention_ffn(nc, x, ctx_in, pos, mask, wq, wk, wv, wo, ffn_w, ffn_bias, gate_w, in_scale, out_scale,
                  rope, out):
    B, S, E = x.shape
    D = 128
    H, KVH = wq.shape[1] // D, wk.shape[1] // D
    HG = H // KVH
    NE = gate_w.shape[0]
    MAXPOS = rope.shape[0]
    P = 128
    EC = E // P
    QT = 4
    TILES = B * S // P
    PAIRS = TILES // QT
    BT = PAIRS * P
    SLOTS = QT * KVH
    KQ = 1 + HG
    PROJ = KQ + 1
    CH = PROJ + HG
    RING = 5
    WRING = 3
    TJ = 2
    SCALE = float(D) ** -0.5
    MASKED = -1.0e9 / SCALE
    EPS = 1e-5
    STREAM = [0, 1, 2, 3, 6, 4, 7, 5, 8, 9]
    PLACE = [STREAM.index(c) for c in range(CH)]
    assert CH % RING == 0 and PROJ % WRING == 0 and BT == 512 and 2 * S == P and KVH == TJ + PAIRS + 2

    x_t = x.rearrange("(n b) s e -> n (b s) e", b=2)
    ctx_t = ctx_in.rearrange("(n b) s e -> n (b s) e", b=2)
    out_t = out.rearrange("(n b) s e -> n (b s) e", b=2)
    mask_t = mask.rearrange("(n b) s t -> n s b t", b=2)
    wq_c = wq.rearrange("(c p) n -> p c n", p=P)
    wk_c = wk.rearrange("(c p) n -> p c n", p=P)
    wv_c = wv.rearrange("(c p) n -> p c n", p=P)

    stack = ExitStack()
    with stack:
        def sb(name, shape, dt=F32):
            return stack.enter_context(nc.sbuf_tensor(name, shape, dt))

        def sem(name):
            return stack.enter_context(nc.semaphore(name))

        xT_hi, xT_lo = (sb(n, [P, EC, 2 * BT], F32R) for n in ("xT_hi", "xT_lo"))
        cT_hi, cT_lo = (sb(n, [P, EC, 2 * BT], F32R) for n in ("cT_hi", "cT_lo"))
        acc = sb("acc", [P, 2 * PAIRS, E])
        cosT, sinT = sb("cosT", [P, 2 * BT]), sb("sinT", [P, 2 * BT])
        w_hi, w_lo = (sb(n, [P, WRING, EC, P], F32R) for n in ("w_hi", "w_lo"))
        wo_hi, wo_lo = (sb(n, [P, HG, E], F32R) for n in ("wo_hi", "wo_lo"))
        raw = sb("raw", [P, RING, E])
        qT = sb("qT", [P, HG // 2, 2 * BT])
        kT = sb("kT", [P, BT])
        vT = sb("vT", [P, BT])
        v = sb("v", [P, PAIRS, D])
        oT_hi, oT_lo = (sb(n, [P, PAIRS, HG, P], F32R) for n in ("oT_hi", "oT_lo"))
        scores = sb("scores", [P, PAIRS, 2 * P])
        msk = sb("msk", [P, PAIRS, P], I32)
        probs = sb("probs", [P, 2, 2, 2, S])
        pT = sb("pT", [P, 2, 2, 2 * P])
        swp = sb("swp", [P, 2, BT])
        rot = sb("rot", [P, 2, BT])
        ident = sb("ident", [P, P])
        smax = sb("smax", [P, 2, 4])
        ssum = sb("ssum", [P, 2, 4])
        srec = sb("srec", [P, 2, 4])
        c_tile, x_tile, f_tile, fT = (sb(n, [P, E]) for n in ("c_tile", "x_tile", "f_tile", "fT"))
        rows = sb("rows", [P, 2 * P])
        pos_i = sb("pos_i", [P, TILES], I32)
        pos_f, pos_w = sb("pos_f", [P, TILES]), sb("pos_w", [P, TILES])
        pos_one = sb("pos_one", [P, 1], I32)
        half = sb("half", [P, 1])
        x_stat, f_stat = sb("x_stat", [P, 6]), sb("f_stat", [P, 6])
        x_mv, f_mv = sb("x_mv", [P, 2]), sb("f_mv", [P, 2])
        x_var, f_var = sb("x_var", [P, 1]), sb("f_var", [P, 1])
        x_rstd, f_rstd = sb("x_rstd", [P, 1]), sb("f_rstd", [P, 1])
        gateT = sb("gateT", [P, EC, NE])
        sgnT = sb("sgnT", [P, EC, E], F32R)
        in_sc, out_sc = sb("in_sc", [P, E], F32R), sb("out_sc", [P, E], F32R)
        route, routeT = sb("route", [P, P]), sb("routeT", [P, P], F32R)
        rexp = sb("rexp", [P, NE])
        rmax, rsum, rrec = sb("rmax", [P, 1]), sb("rsum", [P, 1]), sb("rrec", [P, 1])
        bias_b = sb("bias_b", [P, E])
        y = sb("y", [P, E])
        xs_hi, xs_lo = sb("xs_hi", [P, E], F32R), sb("xs_lo", [P, E], F32R)
        fw = qT[:, :, :].rearrange("p a (b n) -> p (a b) n", n=E)
        in_raw, out_raw = vT, v[:, :, :].rearrange("p a n -> p (a n)")

        chunk = [stack.enter_context(nc.psum_tensor(f"chunk{i}", [P, 512], F32)) for i in range(3)]
        sc_ps, tr_ps, aux = (stack.enter_context(nc.psum_tensor(n, [P, 512], F32)) for n in ("sc_ps", "tr_ps", "aux"))
        o_ps = [stack.enter_context(nc.psum_tensor(f"o_ps{i}", [P, 512], F32)) for i in range(2)]
        OUT_BANK = [0, 1, 2, 0]
        PROJ_BANK = [1, 2, 0, 1, 2, 1]

        raw_in = [sem(f"raw_in{r}") for r in range(RING)]
        x_in, c_in, rows_in, mask_in, res_in = (sem(n) for n in ("x_in", "c_in", "rows_in", "mask_in", "res_in"))
        pos_in, gate_in, fw_in, sc_in, bias_in = (sem(n) for n in ("pos_in", "gate_in", "fw_in", "sc_in", "bias_in"))
        out_done = sem("out_done")
        waits_passed, ident_ok, zeros_ok, consts = (sem(n) for n in ("waits_passed", "ident_ok", "zeros_ok", "consts"))
        pos1, pos2, gate_tr, gate_ok = (sem(n) for n in ("pos1", "pos2", "gate_tr", "gate_ok"))
        fw_neg, fw_sgn, fw_tr, fw_ok, sc_hi, sc_lo = (sem(n) for n in ("fw_neg", "fw_sgn", "fw_tr", "fw_ok", "sc_hi", "sc_lo"))
        wsplit_hi, wsplit_lo = sem("wsplit_hi"), sem("wsplit_lo")
        proj_done, outproj_done = sem("proj_done"), sem("outproj_done")
        swapped, cos_done, sin_done, roped = sem("swapped"), sem("cos_done"), sem("sin_done"), sem("roped")
        vT_ok, v_tr, v_ok = sem("vT_ok"), sem("v_tr"), sem("v_ok")
        scores_done, masked, maxed, shifted = sem("scores_done"), sem("masked"), sem("maxed"), sem("shifted")
        exped, summed, recd, probs_ok = sem("exped"), sem("summed"), sem("recd"), sem("probs_ok")
        probs_tr, pT_a, pT_b = sem("probs_tr"), sem("pT_a"), sem("pT_b")
        pv_done, o_hi, o_lo, added, fill_ok = (sem(n) for n in ("pv_done", "o_hi", "o_lo", "added", "fill_ok"))
        pos_ok, rows_tr, rope_ok = sem("pos_ok"), sem("rows_tr"), sem("rope_ok")
        x_st1, x_st2, x_st3, x_st4, xn_ok = (sem(n) for n in ("x_st1", "x_st2", "x_st3", "x_st4", "xn_ok"))
        x_tr, x_hi, x_lo, c_tr, c_hi, c_lo = (sem(n) for n in ("x_tr", "x_hi", "x_lo", "c_tr", "c_hi", "c_lo"))
        f_st1, f_st2, f_st3, f_st4, fn_ok = (sem(n) for n in ("f_st1", "f_st2", "f_st3", "f_st4", "fn_ok"))
        fn_tr, fn_T, lg_done, rm_ok, re_ok, rr_ok = (sem(n) for n in ("fn_tr", "fn_T", "lg_done", "rm_ok", "re_ok", "rr_ok"))
        rt_ok, rt_tr, rt_hi, rt_lo = (sem(n) for n in ("rt_ok", "rt_tr", "rt_hi", "rt_lo"))
        isc_done, xs_ok, xs_h, xs_l, osc_done, osc_ok = (sem(n) for n in ("isc_done", "xs_ok", "xs_h", "xs_l", "osc_done", "osc_ok"))
        f_done, biased, y_mul, y_ok = (sem(n) for n in ("f_done", "biased", "y_mul", "y_ok"))

        block = stack.enter_context(nc.Block())

        class Slot:

            def __init__(self, q, g, ffn, intake):
                self.q, self.g = q, g
                self.U = q * KVH + g
                n = self.U if isinstance(self.U, int) else None
                self.proj = n is None or n < SLOTS
                self.attn = n is None or 1 <= n <= SLOTS
                self.wo = n is None or n >= 2
                self.first_attn, self.first_proj = n == 1, n == 0
                self.first_wo = n == 2
                self.after_last = n == SLOTS + 1
                self.ffn, self.intake = ffn, intake
                side = q % 2
                self.side = side
                self.wo_side = side if not isinstance(g, int) or g >= 2 else 1 - side
                self.new_mask = isinstance(g, int) and g == 0 and (n is None or 0 < n < SLOTS)

        def run_slots(eng, slot, intake, ffn):
            intake(0, 0, True)
            with eng.Fori(1, PAIRS) as i:
                intake(i, i, False)
            quarter(eng, slot, 0, False, True)
            with eng.Fori(1, QT - 1) as q:
                quarter(eng, slot, q, True, True)
            quarter(eng, slot, QT - 1, True, False)
            slot(Slot(QT, 0, False, False))
            slot(Slot(QT, 1, False, False))
            if ffn is not None:
                with eng.Fori(0, PAIRS) as i:
                    ffn(i + (TILES - PAIRS), i + PAIRS)

        def quarter(eng, slot, q, has_ffn, has_intake):
            slot(Slot(q, 0, False, False))
            slot(Slot(q, 1, False, False))
            with eng.Fori(TJ, TJ + PAIRS) as g:
                slot(Slot(q, g, has_ffn, has_intake))
            with eng.Fori(TJ + PAIRS, KVH) as g:
                slot(Slot(q, g, False, False))

        def jobs_of(s):
            i = s.g - TJ
            t = ((s.q + 1) * PAIRS + i, (1 - s.side) * PAIRS + i)
            f = ((s.q - 1) * PAIRS + i, (1 - s.side) * PAIRS + i)
            return t, f

        def one(tile):
            return slice(tile, tile + 1) if isinstance(tile, int) else bass.ds(tile, 1)

        def span(start, n):
            return slice(start, start + n) if isinstance(start, int) else bass.ds(start, n)

        def row(buffer, tile):
            return buffer[:, one(tile), :].rearrange("p a n -> p (a n)")

        def row_of(dram, t):
            return dram[bass.ds(t, 1)].rearrange("a p n -> (a p) n")

        def by_chunk(bank):
            return bank[:, :].rearrange("p (c n) -> p c n", n=P)

        def flat(ap):
            return ap.rearrange("p c n -> p (c n)")

        def wait_alone(eng, semaphore, count):
            eng.wait_ge(semaphore, count)
            eng.sem_inc(waits_passed, 1)

        @block.sync
        def _(sp):
            sp.dma_start(pos_i[:, :], pos.rearrange("(n b) s -> (b s) n", b=2),
                         allow_slow_non_contiguous=True).then_inc(pos_in, 16)

            def load_tile(t, first):
                if not first:
                    sp.wait_ge(c_tr, t)
                sp.dma_start(c_tile[:, :], row_of(ctx_t, t)).then_inc(c_in, 16)
                if not first:
                    sp.wait_ge(x_tr, t)
                sp.dma_start(x_tile[:, :], row_of(x_t, t)).then_inc(x_in, 16)

            def load_weights(s):
                for n in range(CH):
                    c, r = STREAM[n], n % RING
                    if c >= PROJ:
                        grp = (s.g + KVH - 1) % KVH if isinstance(s.g, int) else s.g - 1
                    else:
                        grp = s.g
                    if not (s.first_proj and n < RING):
                        sp.wait_ge(wsplit_lo, s.U * CH + n - RING + 1)
                    if c < PROJ:
                        src = (wk_c[:, :, bass.ts(grp, D)] if c == 0 else
                               wv_c[:, :, bass.ts(grp, D)] if c == PROJ - 1 else
                               wq_c[:, :, bass.ts(grp * HG + (c - 1), D)])
                        sp.dma_start(raw[:, r, :].rearrange("p (c n) -> p c n", n=P), src).then_inc(raw_in[r], 16)
                    else:
                        sp.dma_start(raw[:, r, :], wo[bass.ts(grp * HG + (c - PROJ), D), :]).then_inc(raw_in[r], 16)

            def load_mask(q):
                for h in range(2):
                    sp.dma_start(msk[h * S:(h + 1) * S, :, :].rearrange("s n (b t) -> s n b t", b=2),
                                 mask_t[bass.ds(q * PAIRS, PAIRS)].rearrange("n s b t -> s n b t")).then_inc(mask_in, 16)

            def slot(s):
                if s.intake:
                    load_tile(jobs_of(s)[0][0], False)
                if s.proj:
                    load_weights(s)
                if s.new_mask:
                    sp.wait_ge(masked, s.U * PAIRS)
                    load_mask(s.q)
                if not s.proj and s.g == 0:
                    for h in range(HG):
                        n = s.U * CH + h
                        sp.wait_ge(wsplit_lo, n - RING + 1)
                        sp.dma_start(raw[:, n % RING, :], wo[bass.ts((KVH - 1) * HG + h, D), :]).then_inc(raw_in[n % RING], 16)

            def intake(t, place, first):
                if not first:
                    load_tile(t, False)

            load_tile(0, True)
            sp.wait_ge(zeros_ok, 5)
            sp.dma_start(kT[0:NE, :], gate_w).then_inc(gate_in, 16)
            sp.dma_start(fw, ffn_w.rearrange("(c p) n -> p c n", p=P)).then_inc(fw_in, 16)
            for k in range(3):
                sp.dma_start(in_raw[32 * k:32 * k + NE, :], in_scale).then_inc(sc_in, 16)
                sp.dma_start(out_raw[32 * k:32 * k + NE, :], out_scale).then_inc(sc_in, 16)
            sp.dma_start(bias_b[:, :], ffn_bias.rearrange("(a n) -> a n", a=1).to_broadcast([P, E])).then_inc(bias_in, 16)
            load_mask(0)
            sp.dma_start(acc[:, 0:PAIRS, :], x_t[0:PAIRS].rearrange("n p e -> p n e")).then_inc(res_in, 16 * PAIRS)
            run_slots(sp, slot, intake, None)

        @block.gpsimd
        def _(pool):
            nc.gpsimd.memset(ident[:, :], 0.0).then_inc(ident_ok, 1)
            pool.wait_ge(ident_ok, 1)
            nc.gpsimd.affine_select(out=ident[:, :], in_=ident[:, :], compare_op=ALU.not_equal, fill=1.0,
                                    base=0, pattern=[[-1, P]], channel_multiplier=1).then_inc(ident_ok, 1)
            for zeros in (kT[:, :], in_raw[:, :], out_raw, route[:, :], pT[:, :, :, :]):
                nc.gpsimd.memset(zeros, 0.0).then_inc(zeros_ok, 1)
            nc.gpsimd.memset(half[:, :], -0.5).then_inc(consts, 1)
            nc.gpsimd.memset(scores[:, :, :], MASKED).then_inc(fill_ok, 1)
            pool.wait_ge(consts, 1)

            def split_lo(s, n):
                c = STREAM[n] if s.proj else PROJ + n
                pool.wait_ge(wsplit_hi, s.U * CH + n + 1)
                if c < PROJ:
                    hi, lo = flat(w_hi[:, c % WRING, :, :]), flat(w_lo[:, c % WRING, :, :])
                else:
                    hi, lo = wo_hi[:, c - PROJ, :], wo_lo[:, c - PROJ, :]
                nc.gpsimd.tensor_tensor(lo, raw[:, n % RING, :], hi.bitcast(F32), ALU.subtract).then_inc(wsplit_lo, 1)

            def gather(t):
                wait_alone(pool, pos_ok, t + 1)
                nc.gpsimd.indirect_dma_start(rows[:, :], None, rope,
                                             bass.IndirectOffsetOnAxis(ap=pos_one[:, :], axis=0)).then_inc(rows_in, 16)

            def x_root(t):
                pool.wait_ge(x_st3, t + 1)
                nc.gpsimd.tensor_tensor(x_rstd[:, :], x_var[:, :], half[:, :], ALU.pow).then_inc(x_st4, 1)

            def f_root(f):
                pool.wait_ge(f_st3, f + 1)
                nc.gpsimd.tensor_tensor(f_rstd[:, :], f_var[:, :], half[:, :], ALU.pow).then_inc(f_st4, 1)

            def add_bias(f, place):
                pool.wait_ge(fn_ok, f + 1)
                nc.gpsimd.tensor_tensor(row(acc, place), row(acc, place), bias_b[:, :], ALU.add).then_inc(biased, 1)

            def slot(s):
                t, f = jobs_of(s) if s.ffn or s.intake else (None, None)
                if s.intake:
                    gather(t[0])
                    x_root(t[0])
                if s.ffn:
                    f_root(f[0])
                if s.proj:
                    for n in range(3):
                        split_lo(s, n)
                if s.ffn:
                    add_bias(*f)
                if s.proj:
                    for n in range(3, CH):
                        split_lo(s, n)
                if s.new_mask:
                    wait_alone(pool, shifted, s.U * PAIRS)
                    nc.gpsimd.memset(scores[:, :, :], MASKED).then_inc(fill_ok, 1)
                if not s.proj and s.g == 0:
                    for n in range(HG):
                        split_lo(s, n)

            def intake(t, place, first):
                gather(t)
                x_root(t)

            def ffn(f, place):
                f_root(f)
                add_bias(f, place)

            def start():
                pool.wait_ge(bias_in, 16)

            start()
            run_slots(pool, slot, intake, ffn)

        @block.scalar
        def _(act):
            def copy(dst, src):
                return nc.scalar.activation(dst, src, ACT.Copy)

            def split_hi(s, n):
                c = STREAM[n] if s.proj else PROJ + n
                r = n % RING
                act.wait_ge(raw_in[r], 16 * ((CH // RING) * s.U + n // RING + 1))
                if c < PROJ:
                    if not (s.first_proj and c < WRING):
                        act.wait_ge(proj_done, s.U * PROJ + c - WRING + 1)
                    hi = flat(w_hi[:, c % WRING, :, :])
                else:
                    if s.wo:
                        act.wait_ge(outproj_done, (s.U - 1) * PAIRS)
                    hi = wo_hi[:, c - PROJ, :]
                copy(hi, raw[:, r, :]).then_inc(wsplit_hi, 1)

            def v_in_rows(s):
                act.wait_ge(v_tr, s.U)
                if not s.first_attn:
                    act.wait_ge(pv_done, (s.U - 1) * PAIRS)
                copy(v[:, :, :].rearrange("p a n -> p (a n)"), tr_ps[:, :]).then_inc(v_ok, 1)

            def exp_pair(s, p):
                act.wait_ge(shifted, (s.U - 1) * PAIRS + p + 1)
                e = probs[:, p % 2, :, :, :].rearrange("p a b t -> p (a b t)")
                nc.scalar.activation(e, e, ACT.Exp, scale=SCALE).then_inc(exped, 1)

            def pT_first(s, p):
                n = (s.U - 1) * PAIRS + p
                act.wait_ge(probs_tr, n + 1)
                if not (s.first_attn and p < 2):
                    act.wait_ge(pv_done, n - 1)
                copy(pT[0:S, p % 2, 0, :], tr_ps[0:S, 0:2 * P]).then_inc(pT_a, 1)

            def out_hi(s, p):
                act.wait_ge(pv_done, (s.U - 1) * PAIRS + p + 1)
                if not s.first_attn:
                    act.wait_ge(outproj_done, (s.U - 2) * PAIRS + p + 1)
                copy(oT_hi[:, p, :, :].rearrange("p h (b s) -> p b h s", b=2),
                     o_ps[p % 2][:, :].rearrange("p (b h s) -> p b h s", b=2, h=HG)).then_inc(o_hi, 1)

            def swap(s, j):
                bank = chunk[PROJ_BANK[j]]
                act.wait_ge(proj_done, s.U * PROJ + j + 1)
                if j >= 2:
                    act.wait_ge(roped, s.U * KQ + j - 1)
                elif not s.first_proj:
                    act.wait_ge(roped, s.U * KQ - j)
                b = swp[:, j % 2, :]
                copy(b[0:D // 2, :], bank[D // 2:D, :])
                copy(b[D // 2:D, :], bank[0:D // 2, :]).then_inc(swapped, 1)

            def v_out(s):
                act.wait_ge(proj_done, (s.U + 1) * PROJ)
                if not s.first_proj:
                    act.wait_ge(v_tr, s.U)
                copy(vT[:, :], chunk[PROJ_BANK[PROJ - 1]][:, :]).then_inc(vT_ok, 1)

            def c_split(t, place):
                act.wait_ge(c_tr, t + 1)
                copy(cT_hi[:, :, span(place * P, P)], by_chunk(aux)).then_inc(c_hi, 1)

            def rope_tables(t, place):
                act.wait_ge(rows_tr, t + 1)
                copy(cosT[:, span(place * P, P)], aux[:, 0:P])
                copy(sinT[:, span(place * P, P)], aux[:, P:2 * P]).then_inc(rope_ok, 1)

            def x_split(t, place):
                act.wait_ge(x_tr, t + 1)
                copy(xT_hi[:, :, span(place * P, P)], by_chunk(aux)).then_inc(x_hi, 1)

            def f_transposed(f):
                act.wait_ge(fn_tr, f + 1)
                copy(fT[:, :], aux[:, :]).then_inc(fn_T, 1)

            def router_exp(f):
                act.wait_ge(rm_ok, f + 1)
                nc.scalar.activation(rexp[:, :], aux[:, 0:NE], ACT.Exp, bias=rmax[:, :],
                                     accum_out=rsum[:, :]).then_inc(re_ok, 1)

            def route_hi(f):
                act.wait_ge(rt_tr, f + 1)
                copy(routeT[:, :], aux[:, 0:P]).then_inc(rt_hi, 1)

            def xs_split(f):
                act.wait_ge(xs_ok, f + 1)
                copy(xs_hi[:, :], fT[:, :]).then_inc(xs_h, 1)

            def out_scales(f):
                act.wait_ge(osc_done, f + 1)
                act.wait_ge(out_done, 16 * (f + 1))
                copy(y[:, :], aux[:, :]).then_inc(osc_ok, 1)

            def store(f):
                act.wait_ge(y_ok, f + 1)
                nc.scalar.dma_start(row_of(out_t, f), y[:, :]).then_inc(out_done, 16)

            def load_residual(t, place):
                nc.scalar.dma_start(row(acc, place), row_of(x_t, t)).then_inc(res_in, 16)

            def slot(s):
                t, f = jobs_of(s) if s.ffn or s.intake else (None, None)
                if s.attn:
                    v_in_rows(s)
                if s.proj:
                    split_hi(s, 0)
                    split_hi(s, 1)
                if s.attn:
                    exp_pair(s, 0)
                if s.intake:
                    c_split(*t)
                if s.proj:
                    split_hi(s, 2)
                if s.attn:
                    exp_pair(s, 1)
                if s.intake:
                    rope_tables(*t)
                if s.attn:
                    pT_first(s, 0)
                    exp_pair(s, 2)
                if s.intake:
                    x_split(*t)
                if s.attn:
                    pT_first(s, 1)
                    exp_pair(s, 3)
                    out_hi(s, 0)
                if s.ffn:
                    f_transposed(f[0])
                if s.proj:
                    swap(s, 0)
                    split_hi(s, 3)
                if s.attn:
                    pT_first(s, 2)
                    out_hi(s, 1)
                if s.ffn:
                    router_exp(f[0])
                if s.proj:
                    split_hi(s, 4)
                    swap(s, 1)
                    split_hi(s, 5)
                if s.attn:
                    pT_first(s, 3)
                    out_hi(s, 2)
                if s.ffn:
                    route_hi(f[0])
                if s.proj:
                    split_hi(s, 6)
                    swap(s, 2)
                    split_hi(s, 7)
                if s.attn:
                    out_hi(s, 3)
                if s.ffn:
                    xs_split(f[0])
                if s.proj:
                    swap(s, 3)
                if s.ffn:
                    out_scales(f[0])
                if s.proj:
                    split_hi(s, 8)
                    swap(s, 4)
                    split_hi(s, 9)
                    v_out(s)
                if not s.proj and s.g == 0:
                    for n in range(HG):
                        split_hi(s, n)
                if s.ffn:
                    store(f[0])
                if s.intake:
                    load_residual(*t)

            def intake(t, place, first):
                c_split(t, place)
                rope_tables(t, place)
                x_split(t, place)

            def ffn(f, place):
                f_transposed(f)
                router_exp(f)
                route_hi(f)
                xs_split(f)
                out_scales(f)
                store(f)

            def start():
                act.wait_ge(gate_tr, 1)
                copy(gateT[:, :, :], by_chunk(aux)[:, :, 0:NE]).then_inc(gate_ok, 1)
                for c in range(EC):
                    act.wait_ge(fw_tr, c + 1)
                    copy(sgnT[:, c, :], chunk[c % 3][:, :]).then_inc(fw_ok, 1)
                act.wait_ge(sc_in, 16 * 6)
                copy(in_sc[:, :], in_raw[:, :]).then_inc(sc_hi, 1)
                copy(out_sc[:, :], out_raw).then_inc(sc_hi, 1)

            start()
            act.sem_inc(out_done, 16)
            run_slots(act, slot, intake, ffn)
            act.wait_ge(out_done, 16 * (TILES + 1))

        @block.vector
        def _(dve):
            def lo_of(dst, src, hi):
                return nc.vector.tensor_tensor(dst, src, hi.bitcast(F32), ALU.subtract)

            def add_out(s, p):
                dve.wait_ge(outproj_done, (s.U - 2) * PAIRS + p + 1)
                a = row(acc, s.wo_side * PAIRS + p)
                nc.vector.tensor_tensor(a, chunk[OUT_BANK[p]][:, :], a, ALU.add).then_inc(added, 1)

            def soft_a(s, p):
                n = (s.U - 1) * PAIRS + p
                if p == 0 and isinstance(s.g, int) and s.g == 1:
                    dve.wait_ge(mask_in, 32 * (s.q + 1))
                    dve.wait_ge(fill_ok, s.q + 1)
                wait_alone(dve, scores_done, n + 1)
                nc.vector.copy_predicated(
                    scores[:, p, :].rearrange("p (a n) -> p a n", a=2),
                    msk[:, p, :].unsqueeze(1).to_broadcast([P, 2, P]),
                    sc_ps[:, 0:2 * P].rearrange("p (a n) -> p a n", a=2)).then_inc(masked, 1)
                dve.wait_ge(masked, n + 1)
                mx = smax[:, p % 2, :]
                sc = scores[:, p, :].rearrange("p (a t) -> p a t", t=S)
                nc.vector.tensor_reduce(mx, sc, AX.X, ALU.max).then_inc(maxed, 1)
                dve.wait_ge(maxed, n + 1)
                if not (s.first_attn and p < 2):
                    dve.wait_ge(probs_tr, n - 1)
                nc.vector.tensor_tensor(probs[:, p % 2, :, :, :].rearrange("p a b t -> p (a b) t"), sc,
                                        mx.unsqueeze(2).to_broadcast([P, 4, S]), ALU.subtract).then_inc(shifted, 1)

            def soft_b(s, p):
                n = (s.U - 1) * PAIRS + p
                e = probs[:, p % 2, :, :, :].rearrange("p a b t -> p (a b) t")
                dve.wait_ge(exped, n + 1)
                nc.vector.tensor_reduce(ssum[:, p % 2, :], e, AX.X, ALU.add).then_inc(summed, 1)
                dve.wait_ge(summed, n + 1)
                nc.vector.reciprocal(srec[:, p % 2, :], ssum[:, p % 2, :]).then_inc(recd, 1)
                dve.wait_ge(recd, n + 1)
                nc.vector.tensor_tensor(e, e, srec[:, p % 2, :].unsqueeze(2).to_broadcast([P, 4, S]),
                                        ALU.mult).then_inc(probs_ok, 1)

            def pT_second(s, p):
                n = (s.U - 1) * PAIRS + p
                dve.wait_ge(probs_tr, n + 1)
                if not (s.first_attn and p < 2):
                    dve.wait_ge(pv_done, n - 1)
                nc.vector.tensor_copy(pT[S:P, p % 2, 1, :], tr_ps[S:P, 0:2 * P]).then_inc(pT_b, 1)

            def out_lo(s, p):
                dve.wait_ge(o_hi, (s.U - 1) * PAIRS + p + 1)
                lo_of(oT_lo[:, p, :, :].rearrange("p h (b s) -> p b h s", b=2),
                      o_ps[p % 2][:, :].rearrange("p (b h s) -> p b h s", b=2, h=HG),
                      oT_hi[:, p, :, :].rearrange("p h (b s) -> p b h s", b=2)).then_inc(o_lo, 1)

            def rotate(s, j):
                n = s.U * KQ + j
                k = j % 2
                here = span(s.side * BT, BT)
                dve.wait_ge(swapped, n + 1)
                nc.vector.tensor_tensor(rot[:, k, :], chunk[PROJ_BANK[j]][:, :], cosT[:, here], ALU.mult).then_inc(cos_done, 1)
                nc.vector.tensor_tensor(swp[:, k, :], swp[:, k, :], sinT[:, here], ALU.mult).then_inc(sin_done, 1)
                if s.attn and j == 0:
                    dve.wait_ge(scores_done, s.U * PAIRS)
                dve.wait_ge(cos_done, n + 1)
                dve.wait_ge(sin_done, n + 1)
                if j == 0:
                    dst, a, b = kT[:, :], rot[:, k, :], swp[:, k, :]
                else:
                    h = j - 1
                    dst = qT[:, h // 2, :].rearrange("p (b a s) -> p b a s", a=2, s=S)[:, :, h % 2, :]
                    a = rot[:, k, :].rearrange("p (b s) -> p b s", s=S)
                    b = swp[:, k, :].rearrange("p (b s) -> p b s", s=S)
                nc.vector.tensor_tensor(dst, a, b, ALU.add).then_inc(roped, 1)

            def pick_positions(t, first=False):
                if not first:
                    dve.wait_ge(rows_tr, t)
                nc.vector.tensor_scalar(pos_one[:, :], pos_f[:, one(t)], 0.0, float(MAXPOS - 1), ALU.max, ALU.min).then_inc(pos_ok, 1)

            def tile_stats(src, stat, mv, var, st1, st2, st3, n):
                nc.vector.bn_stats(stat[:, :], src).then_inc(st1, 1)
                wait_alone(dve, st1, n + 1)
                nc.vector.bn_aggr(mv[:, :], stat[:, :]).then_inc(st2, 1)
                dve.wait_ge(st2, n + 1)
                nc.vector.tensor_scalar(var[:, :], mv[:, 1:2], EPS, None, ALU.add).then_inc(st3, 1)

            def x_stats(t):
                dve.wait_ge(x_in, 16 * (t + 1))
                tile_stats(x_tile[:, :], x_stat, x_mv, x_var, x_st1, x_st2, x_st3, t)

            def x_norm(t):
                dve.wait_ge(x_st4, t + 1)
                nc.vector.tensor_scalar(x_tile[:, :], x_tile[:, :], x_mv[:, 0:1], x_rstd[:, :],
                                        ALU.subtract, ALU.mult).then_inc(xn_ok, 1)

            def c_lo_split(t, place):
                dve.wait_ge(c_hi, t + 1)
                lo_of(cT_lo[:, :, span(place * P, P)], by_chunk(aux), cT_hi[:, :, span(place * P, P)]).then_inc(c_lo, 1)

            def x_lo_split(t, place):
                dve.wait_ge(x_hi, t + 1)
                lo_of(xT_lo[:, :, span(place * P, P)], by_chunk(aux), xT_hi[:, :, span(place * P, P)]).then_inc(x_lo, 1)

            def f_stats(f, place):
                tile_stats(row(acc, place), f_stat, f_mv, f_var, f_st1, f_st2, f_st3, f)

            def f_norm(f, place):
                dve.wait_ge(f_st4, f + 1)
                nc.vector.tensor_scalar(f_tile[:, :], row(acc, place), f_mv[:, 0:1], f_rstd[:, :],
                                        ALU.subtract, ALU.mult).then_inc(fn_ok, 1)

            def router_max(f):
                dve.wait_ge(lg_done, f + 1)
                nc.vector.tensor_reduce(rmax[:, :], aux[:, 0:NE], AX.X, ALU.max, negate=True).then_inc(rm_ok, 1)

            def routing(f):
                dve.wait_ge(re_ok, f + 1)
                nc.vector.reciprocal(rrec[:, :], rsum[:, :]).then_inc(rr_ok, 1)
                dve.wait_ge(rr_ok, f + 1)
                nc.vector.tensor_scalar(route[:, 0:96].rearrange("p (a n) -> p a n", n=32)[:, :, 0:NE],
                                        rexp[:, :].unsqueeze(1).to_broadcast([P, 3, NE]), rrec[:, :], None,
                                        ALU.mult).then_inc(rt_ok, 1)

            def route_lo(f):
                dve.wait_ge(rt_hi, f + 1)
                lo_of(routeT[64:96, :], aux[64:96, 0:P], routeT[64:96, :]).then_inc(rt_lo, 1)

            def scale_in(f):
                dve.wait_ge(isc_done, f + 1)
                nc.vector.tensor_tensor(fT[:, :], aux[:, :], fT[:, :], ALU.mult).then_inc(xs_ok, 1)

            def xs_lo_split(f):
                dve.wait_ge(xs_h, f + 1)
                lo_of(xs_lo[:, :], fT[:, :], xs_hi[:, :]).then_inc(xs_l, 1)

            def finish(f, place):
                dve.wait_ge(f_done, f + 1)
                dve.wait_ge(osc_ok, f + 1)
                nc.vector.tensor_tensor(y[:, :], aux[:, :], y[:, :], ALU.mult).then_inc(y_mul, 1)
                dve.wait_ge(y_mul, f + 1)
                dve.wait_ge(biased, f + 1)
                nc.vector.tensor_tensor(y[:, :], y[:, :], row(acc, place), ALU.add).then_inc(y_ok, 1)

            def slot(s):
                t, f = jobs_of(s) if s.ffn or s.intake else (None, None)
                if s.intake:
                    pick_positions(t[0])
                    x_stats(t[0])
                if s.ffn:
                    dve.wait_ge(added, s.q * KVH * PAIRS)
                    f_stats(*f)
                if s.wo:
                    add_out(s, 0)
                if s.intake:
                    x_norm(t[0])
                if s.attn:
                    soft_a(s, 0)
                if s.ffn:
                    f_norm(*f)
                if s.intake:
                    c_lo_split(*t)
                if s.wo:
                    add_out(s, 1)
                if s.attn:
                    soft_b(s, 0)
                    soft_a(s, 1)
                if s.wo:
                    add_out(s, 2)
                if s.attn:
                    soft_b(s, 1)
                    soft_a(s, 2)
                    pT_second(s, 0)
                if s.intake:
                    x_lo_split(*t)
                if s.wo:
                    add_out(s, 3)
                if s.attn:
                    soft_b(s, 2)
                    soft_a(s, 3)
                    pT_second(s, 1)
                    soft_b(s, 3)
                    out_lo(s, 0)
                    pT_second(s, 2)
                if s.proj:
                    rotate(s, 0)
                if s.attn:
                    out_lo(s, 1)
                if s.ffn:
                    router_max(f[0])
                    routing(f[0])
                if s.attn:
                    pT_second(s, 3)
                if s.proj:
                    rotate(s, 1)
                if s.attn:
                    out_lo(s, 2)
                if s.ffn:
                    route_lo(f[0])
                if s.proj:
                    rotate(s, 2)
                if s.ffn:
                    scale_in(f[0])
                if s.attn:
                    out_lo(s, 3)
                if s.ffn:
                    xs_lo_split(f[0])
                if s.proj:
                    rotate(s, 3)
                if s.ffn:
                    finish(*f)
                if s.proj:
                    rotate(s, 4)
                if isinstance(s.g, int) and s.g == 1 and s.proj:
                    wait_alone(dve, res_in, 16 * PAIRS * (s.q + 1))

            def intake(t, place, first):
                pick_positions(t, first)
                x_stats(t)
                x_norm(t)
                c_lo_split(t, place)
                x_lo_split(t, place)

            def ffn(f, place):
                f_stats(f, place)
                f_norm(f, place)
                router_max(f)
                routing(f)
                route_lo(f)
                scale_in(f)
                xs_lo_split(f)
                finish(f, place)

            def start():
                dve.wait_ge(zeros_ok, 5)
                dve.wait_ge(pos_in, 16)
                nc.vector.tensor_copy(pos_f[:, :], pos_i[:, :]).then_inc(pos1, 1)
                dve.wait_ge(pos1, 1)
                nc.vector.tensor_scalar(pos_w[:, :], pos_f[:, :], 0.0, float(MAXPOS), ALU.is_lt, ALU.mult).then_inc(pos2, 1)
                dve.wait_ge(pos2, 1)
                nc.vector.tensor_tensor(pos_f[:, :], pos_f[:, :], pos_w[:, :], ALU.add).then_inc(pos1, 1)
                dve.wait_ge(pos1, 2)
                dve.wait_ge(fw_in, 16)
                for c in range(EC):
                    if c >= 2:
                        dve.wait_ge(fw_sgn, c - 1)
                    nc.vector.tensor_scalar(rot[:, c % 2, :], fw[:, c, :], 0.0, None, ALU.is_lt).then_inc(fw_neg, 1)
                    dve.wait_ge(fw_neg, c + 1)
                    nc.vector.scalar_tensor_tensor(fw[:, c, :], fw[:, c, :], 0.0, rot[:, c % 2, :],
                                                   ALU.is_gt, ALU.subtract).then_inc(fw_sgn, 1)
                dve.wait_ge(sc_hi, 2)
                lo_of(in_sc[32:64, :], in_raw[32:64, :], in_sc[32:64, :]).then_inc(sc_lo, 1)
                lo_of(out_sc[32:64, :], out_raw[32:64, :], out_sc[32:64, :]).then_inc(sc_lo, 1)

            start()
            run_slots(dve, slot, intake, ffn)

        @block.tensor
        def _(pe):
            def transpose(dst, src):
                return nc.tensor.transpose(dst, src, ident[:, :])

            def transpose_tile(src):
                for c in range(EC):
                    last = transpose(aux[:, bass.ts(c, P)], src[:, bass.ts(c, P)])
                return last

            def split_products(bank, operands):
                last, n = None, len(operands)
                for i, (a_hi, a_lo, b_hi, b_lo) in enumerate(operands):
                    nc.tensor.matmul(bank, a_hi, b_hi, start=i == 0, stop=False)
                    nc.tensor.matmul(bank, a_hi, b_lo, start=False, stop=False)
                    last = nc.tensor.matmul(bank, a_lo, b_hi, start=False, stop=i == n - 1)
                return last

            def out_proj(s, p):
                n = (s.U - 2) * PAIRS + p
                if p == 3:
                    pe.wait_ge(added, n - 2)
                elif s.after_last:
                    pe.wait_ge(added, (s.U - 3) * PAIRS + (4 if p == 0 else p + 1))
                elif p == 0:
                    pe.wait_ge(cos_done, (s.U - 1) * KQ + 3)
                elif p == 1:
                    pe.wait_ge(vT_ok, s.U)
                else:
                    pe.wait_ge(cos_done, (s.U - 1) * KQ + 5)
                if p == 0:
                    pe.wait_ge(wsplit_lo, SLOTS * CH + HG if s.after_last else s.U * CH)
                pe.wait_ge(o_lo, n + 1)
                split_products(chunk[OUT_BANK[p]][:, :],
                               [(oT_hi[:, p, h, :], oT_lo[:, p, h, :], wo_hi[:, h, :], wo_lo[:, h, :])
                                for h in range(HG)]).then_inc(outproj_done, 1)

            def v_rows(s):
                pe.wait_ge(vT_ok, s.U)
                if not s.first_attn:
                    pe.wait_ge(pT_a, (s.U - 1) * PAIRS)
                    pe.wait_ge(pT_b, (s.U - 1) * PAIRS)
                for p in range(PAIRS):
                    last = transpose(tr_ps[:, bass.ts(p, D)], vT[:, bass.ts(p, P)])
                last.then_inc(v_tr, 1)

            def scores_of(s, p):
                n = (s.U - 1) * PAIRS + p
                pe.wait_ge(roped, s.U * KQ)
                if not (s.first_attn and p == 0):
                    pe.wait_ge(masked, n)
                for hp in range(HG // 2):
                    for b in range(2):
                        at = 2 * p + b
                        last = nc.tensor.matmul(sc_ps[:, bass.ts(2 * hp + b, S)], qT[:, hp, bass.ts(at, P)],
                                                kT[:, bass.ts(at, S)], start=True, stop=True)
                last.then_inc(scores_done, 1)

            def probs_T(s, p):
                n = (s.U - 1) * PAIRS + p
                pe.wait_ge(probs_ok, n + 1)
                if p == 0:
                    pe.wait_ge(v_ok, s.U)
                else:
                    pe.wait_ge(pT_a, n)
                    pe.wait_ge(pT_b, n)
                for hp in range(2):
                    last = transpose(tr_ps[:, bass.ts(hp, P)], probs[:, p % 2, hp, :, :].rearrange("p b t -> p (b t)"))
                last.then_inc(probs_tr, 1)

            def values(s, p):
                n = (s.U - 1) * PAIRS + p
                pe.wait_ge(pT_a, n + 1)
                pe.wait_ge(pT_b, n + 1)
                if not (s.first_attn and p < 2):
                    pe.wait_ge(o_lo, n - 1)
                nc.tensor.matmul(o_ps[p % 2][:, :], v[:, p, :], pT[:, p % 2, :, :].rearrange("p b n -> p (b n)"),
                                 start=True, stop=True).then_inc(pv_done, 1)

            def project(s, j):
                if s.first_proj and j == 0:
                    pe.wait_ge(x_lo, PAIRS)
                if j < 3 and s.wo:
                    pe.wait_ge(added, (s.U - 2) * PAIRS + 2 + j)
                elif j == 0 and not s.first_proj:
                    pe.wait_ge(vT_ok, s.U)
                elif j == 1 and not s.first_proj:
                    pe.wait_ge(cos_done, s.U * KQ)
                elif j == 2 and not s.first_proj:
                    pe.wait_ge(cos_done, (s.U - 1) * KQ + 3)
                elif j >= 3:
                    pe.wait_ge(cos_done, s.U * KQ + [1, 2, 4][j - 3])
                pe.wait_ge(wsplit_lo, s.U * CH + PLACE[j] + 1)
                src_hi, src_lo = (xT_hi, xT_lo) if 0 < j < PROJ - 1 else (cT_hi, cT_lo)
                here = span(s.side * BT, BT)
                split_products(chunk[PROJ_BANK[j]][:, :],
                               [(w_hi[:, j % WRING, c, :], w_lo[:, j % WRING, c, :], src_hi[:, c, here], src_lo[:, c, here])
                                for c in range(EC)]).then_inc(proj_done, 1)

            def t_context(t, alone, first=False):
                if alone and not first:
                    pe.wait_ge(x_lo, t)
                pe.wait_ge(c_in, 16 * (t + 1))
                transpose_tile(c_tile).then_inc(c_tr, 1)

            def t_rows(t):
                pe.wait_ge(c_lo, t + 1)
                pe.wait_ge(rows_in, 16 * (t + 1))
                transpose(aux[:, 0:P], rows[:, 0:P])
                transpose(aux[:, P:2 * P], rows[:, P:2 * P]).then_inc(rows_tr, 1)

            def t_x(t):
                pe.wait_ge(rope_ok, t + 1)
                pe.wait_ge(xn_ok, t + 1)
                transpose_tile(x_tile).then_inc(x_tr, 1)

            def t_f(f, t, alone):
                if t is not None:
                    pe.wait_ge(x_lo, t + 1)
                elif alone:
                    pe.wait_ge(y_mul, f)
                pe.wait_ge(fn_ok, f + 1)
                transpose_tile(f_tile).then_inc(fn_tr, 1)

            def t_logits(f):
                pe.wait_ge(fn_T, f + 1)
                for c in range(EC):
                    last = nc.tensor.matmul(aux[:, 0:NE], fT[:, bass.ts(c, P)], gateT[:, c, :],
                                            start=c == 0, stop=c == EC - 1)
                last.then_inc(lg_done, 1)

            def t_route(f):
                pe.wait_ge(rt_ok, f + 1)
                transpose(aux[:, 0:P], route[:, :]).then_inc(rt_tr, 1)

            def t_in_scales(f):
                pe.wait_ge(rt_lo, f + 1)
                for c in range(EC):
                    last = nc.tensor.matmul(aux[:, bass.ts(c, P)], in_sc[:, bass.ts(c, P)], routeT[:, :],
                                            start=True, stop=True)
                last.then_inc(isc_done, 1)

            def t_out_scales(f):
                pe.wait_ge(xs_ok, f + 1)
                nc.tensor.matmul(aux[:, :], routeT[:, :], out_sc[:, :], start=True, stop=True).then_inc(osc_done, 1)

            def t_product(f):
                pe.wait_ge(osc_ok, f + 1)
                pe.wait_ge(xs_l, f + 1)
                for c in range(EC):
                    nc.tensor.matmul(aux[:, :], xs_hi[:, bass.ts(c, P)], sgnT[:, c, :], start=c == 0, stop=False)
                    last = nc.tensor.matmul(aux[:, :], xs_lo[:, bass.ts(c, P)], sgnT[:, c, :],
                                            start=False, stop=c == EC - 1)
                last.then_inc(f_done, 1)

            def slot(s):
                (t, _), (f, _) = jobs_of(s) if s.ffn or s.intake else ((None, None), (None, None))
                if s.wo:
                    out_proj(s, 0)
                if s.attn:
                    v_rows(s)
                    scores_of(s, 0)
                if s.intake:
                    t_context(t, False)
                if s.wo:
                    out_proj(s, 1)
                if s.attn:
                    scores_of(s, 1)
                if s.intake:
                    t_rows(t)
                if s.wo:
                    out_proj(s, 2)
                if s.attn:
                    scores_of(s, 2)
                    probs_T(s, 0)
                if s.intake:
                    t_x(t)
                if s.wo:
                    out_proj(s, 3)
                if s.attn:
                    scores_of(s, 3)
                    probs_T(s, 1)
                    values(s, 0)
                if s.ffn:
                    t_f(f, t if s.intake else None, False)
                if s.proj:
                    project(s, 0)
                if s.attn:
                    probs_T(s, 2)
                    values(s, 1)
                if s.ffn:
                    t_logits(f)
                if s.proj:
                    project(s, 1)
                if s.attn:
                    probs_T(s, 3)
                    values(s, 2)
                if s.ffn:
                    t_route(f)
                if s.proj:
                    project(s, 2)
                if s.attn:
                    values(s, 3)
                if s.ffn:
                    t_in_scales(f)
                if s.proj:
                    project(s, 3)
                if s.ffn:
                    t_out_scales(f)
                if s.proj:
                    project(s, 4)
                if s.ffn:
                    t_product(f)
                if s.proj:
                    project(s, 5)

            def intake(t, place, first):
                t_context(t, True, first)
                t_rows(t)
                t_x(t)

            def ffn(f, place):
                t_f(f, None, True)
                t_logits(f)
                t_route(f)
                t_in_scales(f)
                t_out_scales(f)
                t_product(f)

            def start():
                pe.wait_ge(ident_ok, 2)
                pe.wait_ge(gate_in, 16)
                transpose_tile(kT).then_inc(gate_tr, 1)
                pe.wait_ge(gate_ok, 1)
                for c in range(EC):
                    pe.wait_ge(fw_sgn, EC)
                    if c == 3:
                        pe.wait_ge(fw_ok, 1)
                    for o in range(EC):
                        last = transpose(chunk[c % 3][:, bass.ts(o, P)], fw[:, o, bass.ts(c, P)])
                    last.then_inc(fw_tr, 1)
                pe.wait_ge(fw_ok, EC)
                pe.wait_ge(sc_lo, 2)

            start()
            run_slots(pe, slot, intake, ffn)


_INS = ["x", "ctx_4096", "pos_BxS2", "mask_BxSxS2_ik0", "L0_xattn_Wq", "L0_xattn_Wk", "L0_xattn_Wv", "L0_xattn_Wo",
        "L0_ffn_weight", "L0_ffn_bias", "L0_ffn_gate_w", "L0_ffn_in_channel_scale", "L0_ffn_out_channel_scale"]


def rope_table(positions=512, dim=128, theta=10000.0):
    import numpy as np
    inv = (1.0 / np.float32(theta) ** (np.arange(0, dim, 2, dtype=np.float32) / np.float32(dim))).astype(np.float32)
    angle = np.arange(positions, dtype=np.float32)[:, None] * inv[None, :]
    c, s = np.cos(angle), np.sin(angle)
    return np.concatenate([c, c, -s, s], axis=1).astype(np.float32)


def kernel(**inputs):
    import numpy as np
    import concourse.bacc as bacc
    from concourse.bass_utils import run_bass_kernel_spmd as run

    nc = bacc.Bacc("TRN2", target_bir_lowering=False, num_devices=1)
    arrays = {f"in_{n}": np.ascontiguousarray(inputs[n]) for n in _INS}
    arrays["rope_table"] = rope_table()
    args = [nc.dram_tensor(n, a.shape, mybir.dt.from_np(a.dtype), kind="ExternalInput").ap() for n, a in arrays.items()]
    shape = arrays["in_x"].shape
    args.append(nc.dram_tensor("result", shape, F32, kind="ExternalOutput").ap())
    attention_ffn(nc, *args)
    r = run(nc, [arrays], core_ids=[0])
    return r.results[0]["result"]
```

```python
import concourse.bass as bass
from concourse import mybir
from contextlib import ExitStack

F32 = mybir.dt.float32
F32R = mybir.dt.float32r
I32 = mybir.dt.int32
ALU = mybir.AluOpType
ACT = mybir.ActivationFunctionType
AX = mybir.AxisListType


def attention_ffn(nc, x, ctx_in, pos, mask, wq, wk, wv, wo, ffn_w, ffn_bias, gate_w, in_scale, out_scale,
                  rope, out):
    B, S, E = x.shape
    D = 128
    H, KVH = wq.shape[1] // D, wk.shape[1] // D
    HG = H // KVH
    NE = gate_w.shape[0]
    MAXPOS = rope.shape[0]
    P = 128
    EC = E // P
    QT = 4
    TILES = B * S // P
    PAIRS = TILES // QT
    BT = PAIRS * P
    SLOTS = QT * KVH
    KQ = 1 + HG
    PROJ = KQ + 1
    CH = PROJ + HG
    RING = 5
    WRING = 3
    TJ = 2
    SCALE = float(D) ** -0.5
    MASKED = -1.0e9 / SCALE
    EPS = 1e-5
    STREAM = [0, 1, 2, 3, 6, 4, 7, 5, 8, 9]
    PLACE = [STREAM.index(c) for c in range(CH)]
    assert CH % RING == 0 and PROJ % WRING == 0 and BT == 512 and 2 * S == P and KVH == TJ + PAIRS + 2

    x_t = x.rearrange("(n b) s e -> n (b s) e", b=2)
    ctx_t = ctx_in.rearrange("(n b) s e -> n (b s) e", b=2)
    out_t = out.rearrange("(n b) s e -> n (b s) e", b=2)
    mask_t = mask.rearrange("(n b) s t -> n s b t", b=2)
    wq_c = wq.rearrange("(c p) n -> p c n", p=P)
    wk_c = wk.rearrange("(c p) n -> p c n", p=P)
    wv_c = wv.rearrange("(c p) n -> p c n", p=P)

    stack = ExitStack()
    with stack:
        def sb(name, shape, dt=F32):
            return stack.enter_context(nc.sbuf_tensor(name, shape, dt))

        def sem(name):
            return stack.enter_context(nc.semaphore(name))

        xT_hi, xT_lo = (sb(n, [P, EC, 2 * BT], F32R) for n in ("xT_hi", "xT_lo"))
        cT_hi, cT_lo = (sb(n, [P, EC, 2 * BT], F32R) for n in ("cT_hi", "cT_lo"))
        acc = sb("acc", [P, 2 * PAIRS, E])
        cosT, sinT = sb("cosT", [P, 2 * BT]), sb("sinT", [P, 2 * BT])
        w_hi, w_lo = (sb(n, [P, WRING, EC, P], F32R) for n in ("w_hi", "w_lo"))
        wo_hi, wo_lo = (sb(n, [P, HG, E], F32R) for n in ("wo_hi", "wo_lo"))
        raw = sb("raw", [P, RING, E])
        qT = sb("qT", [P, HG // 2, 2 * BT])
        kT = sb("kT", [P, BT])
        vT = sb("vT", [P, BT])
        v_hi, v_lo = (sb(n, [P, PAIRS, D], F32R) for n in ("v_hi", "v_lo"))
        oT_hi, oT_lo = (sb(n, [P, PAIRS, HG, P], F32R) for n in ("oT_hi", "oT_lo"))
        scores = sb("scores", [P, PAIRS, 2 * P])
        msk = sb("msk", [P, PAIRS, P], I32)
        probs = sb("probs", [P, 2, 2, 2, S])
        pT_hi, pT_lo = (sb(n, [P, 2, 2 * P], F32R) for n in ("pT_hi", "pT_lo"))
        swp = sb("swp", [P, 2, BT])
        rot = sb("rot", [P, BT])
        ident = sb("ident", [P, P])
        smax = sb("smax", [P, 2, 4])
        ssum = sb("ssum", [P, 2, 4])
        srec = sb("srec", [P, 2, 4])
        c_tile, x_tile, f_tile, fT = (sb(n, [P, E]) for n in ("c_tile", "x_tile", "f_tile", "fT"))
        rows = sb("rows", [P, 2 * P])
        pos_i = sb("pos_i", [P, TILES], I32)
        pos_f, pos_w = sb("pos_f", [P, TILES]), sb("pos_w", [P, TILES])
        pos_one, pos_first = sb("pos_one", [P, 1], I32), sb("pos_first", [P, PAIRS], I32)
        s_stat, s_mv = sb("s_stat", [P, PAIRS, 6]), sb("s_mv", [P, PAIRS, 2])
        s_var, s_rstd = sb("s_var", [P, PAIRS]), sb("s_rstd", [P, PAIRS])
        half = sb("half", [P, PAIRS])
        x_stat, f_stat = sb("x_stat", [P, 6]), sb("f_stat", [P, 6])
        x_mv, f_mv = sb("x_mv", [P, 2]), sb("f_mv", [P, 2])
        x_var, f_var = sb("x_var", [P, 1]), sb("f_var", [P, 1])
        x_rstd, f_rstd = sb("x_rstd", [P, 1]), sb("f_rstd", [P, 1])
        gateT = sb("gateT", [P, EC, NE])
        sgnT = sb("sgnT", [P, EC, E], F32R)
        in_sc, out_sc = sb("in_sc", [P, E], F32R), sb("out_sc", [P, E], F32R)
        route, routeT = sb("route", [P, P]), sb("routeT", [P, P], F32R)
        rexp = sb("rexp", [P, NE])
        rmax, rsum, rrec = sb("rmax", [P, 1]), sb("rsum", [P, 1]), sb("rrec", [P, 1])
        bias_b = sb("bias_b", [P, E])
        y = sb("y", [P, E])
        xs_hi, xs_lo = sb("xs_hi", [P, E], F32R), sb("xs_lo", [P, E], F32R)
        four_tiles = qT[:, :, :].rearrange("p a (b n) -> p (a b) n", n=E)
        fw, c_first, rows_first = acc[:, PAIRS:2 * PAIRS, :], four_tiles, scores
        in_raw, out_raw, gate_raw = vT, probs[:, :, :, :, :].rearrange("p k a b t -> p (k a b t)"), c_tile

        chunk = [stack.enter_context(nc.psum_tensor(f"chunk{i}", [P, 512], F32)) for i in range(3)]
        sc_ps, tr_ps, aux = (stack.enter_context(nc.psum_tensor(n, [P, 512], F32)) for n in ("sc_ps", "tr_ps", "aux"))
        o_ps = [stack.enter_context(nc.psum_tensor(f"o_ps{i}", [P, 512], F32)) for i in range(2)]
        C_BANK, X_BANK = [aux, sc_ps, tr_ps, o_ps[0]], [chunk[0], chunk[2], o_ps[1], aux]
        ROWS_BANK, SGN_BANK, GATE_BANK = [sc_ps, tr_ps], [sc_ps, tr_ps, o_ps[0], aux], o_ps[1]
        x_first = [x_tile, f_tile, fT, y]

        class FfnBuffers:

            def __init__(self, stat, mv, var, rstd, bank, tile, tile_T, route, routeT, rexp, rmax, rsum, rrec, xs_hi, xs_lo, y):
                self.stat, self.mv, self.var, self.rstd = stat, mv, var, rstd
                self.bank, self.tile, self.tile_T = bank, tile, tile_T
                self.route, self.routeT, self.rexp = route, routeT, rexp
                self.rmax, self.rsum, self.rrec = rmax, rsum, rrec
                self.xs_hi, self.xs_lo, self.y = xs_hi, xs_lo, y

        in_slot = FfnBuffers(f_stat[:, :], f_mv[:, :], f_var[:, :], f_rstd[:, :], aux[:, :], f_tile[:, :], fT[:, :], route[:, :], routeT[:, :], rexp[:, :],
                             rmax[:, :], rsum[:, :], rrec[:, :], xs_hi[:, :], xs_lo[:, :], y[:, :])
        at_end = [FfnBuffers(s_stat[:, p, :], s_mv[:, p, :], s_var[:, p:p + 1], s_rstd[:, p:p + 1],
                             [aux, sc_ps, tr_ps, o_ps[0]][p][:, :], raw[:, p, :], four_tiles[:, p, :],
                             swp[:, 0, bass.ts(p, P)], cT_hi[:, p, 0:P], rot[:, 32 * p:32 * p + NE],
                             rot[:, P + 4 * p:P + 4 * p + 1], rot[:, P + 4 * p + 1:P + 4 * p + 2],
                             rot[:, P + 4 * p + 2:P + 4 * p + 3],
                             xT_hi[:, p, 0:E], xT_lo[:, p, 0:E],
                             (cosT if p < 2 else sinT)[:, bass.ts(p % 2, E)]) for p in range(PAIRS)]
        OUT_BANK = [0, 1, 2, 0]
        PROJ_BANK = [1, 2, 0, 1, 2, 1]

        raw_in = [sem(f"raw_in{r}") for r in range(RING)]
        x_in, c_in, rows_in, mask_in, res_in = (sem(n) for n in ("x_in", "c_in", "rows_in", "mask_in", "res_in"))
        pos_in, gate_in, fw_in, sc_in, bias_in = (sem(n) for n in ("pos_in", "gate_in", "fw_in", "sc_in", "bias_in"))
        out_done = sem("out_done")
        c_first_in, x_first_in = ([sem(f"{n}{p}") for p in range(PAIRS)] for n in ("c_first_in", "x_first_in"))
        pos_first_ok, rows_first_in, route_ok = sem("pos_first_ok"), sem("rows_first_in"), sem("route_ok")
        waits_passed, ident_ok, zeros_ok, consts = (sem(n) for n in ("waits_passed", "ident_ok", "zeros_ok", "consts"))
        pos1, pos2, gate_tr, gate_ok = (sem(n) for n in ("pos1", "pos2", "gate_tr", "gate_ok"))
        fw_neg, fw_sgn, fw_tr, fw_ok, sc_hi, sc_lo = (sem(n) for n in ("fw_neg", "fw_sgn", "fw_tr", "fw_ok", "sc_hi", "sc_lo"))
        wsplit_hi, wsplit_lo = sem("wsplit_hi"), sem("wsplit_lo")
        proj_done, outproj_done = sem("proj_done"), sem("outproj_done")
        swapped, cos_done, sin_done, roped = sem("swapped"), sem("cos_done"), sem("sin_done"), sem("roped")
        vT_ok, v_tr, v_h, v_ok = sem("vT_ok"), sem("v_tr"), sem("v_h"), sem("v_ok")
        scores_done, masked, maxed, shifted = sem("scores_done"), sem("masked"), sem("maxed"), sem("shifted")
        exped, summed, recd, probs_ok = sem("exped"), sem("summed"), sem("recd"), sem("probs_ok")
        probs_tr, pT_h, pT_l = sem("probs_tr"), sem("pT_h"), sem("pT_l")
        pv_done, o_hi, o_lo, added, fill_ok = (sem(n) for n in ("pv_done", "o_hi", "o_lo", "added", "fill_ok"))
        pos_ok, rows_tr, rope_ok = sem("pos_ok"), sem("rows_tr"), sem("rope_ok")
        x_st1, x_st2, x_st3, x_st4, xn_ok = (sem(n) for n in ("x_st1", "x_st2", "x_st3", "x_st4", "xn_ok"))
        x_tr, x_hi, x_lo, c_tr, c_hi, c_lo = (sem(n) for n in ("x_tr", "x_hi", "x_lo", "c_tr", "c_hi", "c_lo"))
        f_st1, f_st2, f_st3, f_st4, fn_ok = (sem(n) for n in ("f_st1", "f_st2", "f_st3", "f_st4", "fn_ok"))
        fn_tr, fn_T, lg_done, rm_ok, re_ok, rr_ok = (sem(n) for n in ("fn_tr", "fn_T", "lg_done", "rm_ok", "re_ok", "rr_ok"))
        rt_ok, rt_tr, rt_hi, rt_lo = (sem(n) for n in ("rt_ok", "rt_tr", "rt_hi", "rt_lo"))
        isc_done, xs_ok, xs_h, xs_l, osc_done, osc_ok = (sem(n) for n in ("isc_done", "xs_ok", "xs_h", "xs_l", "osc_done", "osc_ok"))
        f_done, biased, y_mul, y_ok = (sem(n) for n in ("f_done", "biased", "y_mul", "y_ok"))

        LAST_STEPS = 8

        block = stack.enter_context(nc.Block())

        class Slot:

            def __init__(self, q, g, ffn, intake, residual=False):
                self.q, self.g = q, g
                self.U = q * KVH + g
                n = self.U if isinstance(self.U, int) else None
                self.number = n
                self.proj = n is None or n < SLOTS
                self.attn = n is None or 1 <= n <= SLOTS
                self.wo = n is None or n >= 2
                self.first_attn, self.first_proj = n == 1, n == 0
                self.after_last = n == SLOTS + 1
                self.ffn, self.intake, self.residual = ffn, intake, residual
                self.side = side = q % 2
                self.wo_side = side if not isinstance(g, int) or g >= 2 else 1 - side
                self.new_mask = isinstance(g, int) and g == 0 and (n is None or 0 < n < SLOTS)

        def last_tile(p):
            return TILES - PAIRS + p, PAIRS + p, at_end[p]

        def run_slots(eng, slot, last_step):
            quarter(eng, slot, 0, False, True)
            with eng.Fori(1, QT - 1) as q:
                quarter(eng, slot, q, True, True)
            quarter(eng, slot, QT - 1, True, False)
            slot(Slot(QT, 0, False, False))
            last_slot = Slot(QT, 1, False, False)
            for turn in range(PAIRS + LAST_STEPS - 1):
                for p in reversed(range(PAIRS)):
                    if 0 <= turn - p < LAST_STEPS:
                        last_step(last_slot, turn - p, p)

        def quarter(eng, slot, q, has_ffn, has_intake):
            first = isinstance(q, int) and q == 0
            slot(Slot(q, 0, False, has_intake and not first))
            slot(Slot(q, 1, False, has_intake and not first))
            with eng.Fori(TJ, TJ + PAIRS) as g:
                slot(Slot(q, g, has_ffn, first, has_intake))
            with eng.Fori(TJ + PAIRS, KVH) as g:
                slot(Slot(q, g, False, has_intake and not first))

        def tile_in(s, i):
            return (s.q + 1) * PAIRS + i, (1 - s.side) * PAIRS + i

        def jobs_of(s):
            i = s.g - TJ
            t = tile_in(s, i if s.residual else s.g if isinstance(s.g, int) else s.g - PAIRS) if s.intake else None
            f = ((s.q - 1) * PAIRS + i, (1 - s.side) * PAIRS + i) if s.ffn else None
            return t, f, tile_in(s, i) if s.residual else None

        def one(tile):
            return slice(tile, tile + 1) if isinstance(tile, int) else bass.ds(tile, 1)

        def span(start, n):
            return slice(start, start + n) if isinstance(start, int) else bass.ds(start, n)

        def row(buffer, tile):
            return buffer[:, one(tile), :].rearrange("p a n -> p (a n)")

        def row_of(dram, t):
            return dram[bass.ds(t, 1)].rearrange("a p n -> (a p) n")

        def by_chunk(bank):
            return bank[:, :].rearrange("p (c n) -> p c n", n=P)

        def flat(ap):
            return ap.rearrange("p c n -> p (c n)")

        def flat2(buffer):
            return buffer[:, :, :].rearrange("p b n -> p (b n)")

        def wait_alone(eng, semaphore, count):
            eng.wait_ge(semaphore, count)
            eng.sem_inc(waits_passed, 1)

        @block.sync
        def _(sp):
            def load_tile(t):
                sp.wait_ge(c_tr, t)
                sp.dma_start(c_tile[:, :], row_of(ctx_t, t)).then_inc(c_in, 16)
                sp.wait_ge(x_tr, t)
                sp.dma_start(x_tile[:, :], row_of(x_t, t)).then_inc(x_in, 16)

            def load_weights(s):
                for n in range(CH):
                    if s.first_proj and n == RING:
                        load_constants()
                    c, r = STREAM[n], n % RING
                    if c >= PROJ:
                        grp = (s.g + KVH - 1) % KVH if isinstance(s.g, int) else s.g - 1
                    else:
                        grp = s.g
                    if not (s.first_proj and n < RING):
                        sp.wait_ge(wsplit_lo, s.U * CH + n - RING + 1)
                    if c < PROJ:
                        src = (wk_c[:, :, bass.ts(grp, D)] if c == 0 else
                               wv_c[:, :, bass.ts(grp, D)] if c == PROJ - 1 else
                               wq_c[:, :, bass.ts(grp * HG + (c - 1), D)])
                        sp.dma_start(raw[:, r, :].rearrange("p (c n) -> p c n", n=P), src).then_inc(raw_in[r], 16)
                    else:
                        sp.dma_start(raw[:, r, :], wo[bass.ts(grp * HG + (c - PROJ), D), :]).then_inc(raw_in[r], 16)

            def load_mask(q):
                for h in range(2):
                    sp.dma_start(msk[h * S:(h + 1) * S, :, :].rearrange("s n (b t) -> s n b t", b=2),
                                 mask_t[bass.ds(q * PAIRS, PAIRS)].rearrange("n s b t -> s n b t")).then_inc(mask_in, 16)

            def load_constants():
                load_mask(0)
                sp.dma_start(fw, ffn_w.rearrange("(c p) n -> p c n", p=P)).then_inc(fw_in, 16)
                sp.wait_ge(zeros_ok, 4)
                sp.dma_start(gate_raw[0:NE, :], gate_w).then_inc(gate_in, 16)
                for k in range(3):
                    sp.dma_start(in_raw[32 * k:32 * k + NE, :], in_scale).then_inc(sc_in, 16)
                    sp.dma_start(out_raw[32 * k:32 * k + NE, :], out_scale).then_inc(sc_in, 16)
                sp.dma_start(bias_b[:, :], ffn_bias.rearrange("(a n) -> a n", a=1).to_broadcast([P, E])).then_inc(bias_in, 16)

            def slot(s):
                if s.number == 1:
                    sp.wait_ge(gate_tr, 1)
                if s.intake:
                    load_tile(jobs_of(s)[0][0])
                if s.proj:
                    load_weights(s)
                if s.new_mask:
                    sp.wait_ge(masked, s.U * PAIRS)
                    load_mask(s.q)
                if s.number == SLOTS:
                    for h in range(HG):
                        n = s.U * CH + h
                        sp.wait_ge(wsplit_lo, n - RING + 1)
                        sp.dma_start(raw[:, n % RING, :], wo[bass.ts((KVH - 1) * HG + h, D), :]).then_inc(raw_in[n % RING], 16)

            sp.dma_start(pos_i[:, :], pos.rearrange("(n b) s -> (b s) n", b=2),
                         allow_slow_non_contiguous=True).then_inc(pos_in, 16)
            for p in range(PAIRS):
                sp.dma_start(c_first[:, p, :], row_of(ctx_t, p)).then_inc(c_first_in[p], 16)
            run_slots(sp, slot, lambda s, step, p: None)

        @block.gpsimd
        def _(pool):
            def gather_rows(dst, positions):
                return nc.gpsimd.indirect_dma_start(dst, None, rope, bass.IndirectOffsetOnAxis(ap=positions, axis=0))

            nc.gpsimd.memset(ident[:, :], 0.0).then_inc(ident_ok, 1)
            pool.wait_ge(ident_ok, 1)
            nc.gpsimd.affine_select(out=ident[:, :], in_=ident[:, :], compare_op=ALU.not_equal, fill=1.0,
                                    base=0, pattern=[[-1, P]], channel_multiplier=1).then_inc(ident_ok, 1)
            nc.gpsimd.memset(half[:, :], -0.5).then_inc(consts, 1)
            wait_alone(pool, pos_first_ok, 1)
            for p in range(PAIRS):
                gather_rows(rows_first[:, p, :], pos_first[:, p:p + 1]).then_inc(rows_first_in, 16)
            for zeros in (gate_raw[:, :], in_raw[:, :], out_raw, route[:, :],
                          pT_hi[:, :, :].bitcast(F32), pT_lo[:, :, :].bitcast(F32)):
                nc.gpsimd.memset(zeros, 0.0).then_inc(zeros_ok, 1)
            pool.wait_ge(consts, 1)
            pool.wait_ge(x_st3, PAIRS)
            nc.gpsimd.tensor_tensor(s_rstd[:, :], s_var[:, :], half[:, :], ALU.pow).then_inc(x_st4, PAIRS)

            def split_lo(s, n):
                c = STREAM[n] if s.proj else PROJ + n
                pool.wait_ge(wsplit_hi, s.U * CH + n + 1)
                if c < PROJ:
                    hi, lo = flat(w_hi[:, c % WRING, :, :]), flat(w_lo[:, c % WRING, :, :])
                else:
                    hi, lo = wo_hi[:, c - PROJ, :], wo_lo[:, c - PROJ, :]
                nc.gpsimd.tensor_tensor(lo, raw[:, n % RING, :], hi.bitcast(F32), ALU.subtract).then_inc(wsplit_lo, 1)

            def gather(t):
                wait_alone(pool, pos_ok, t + 1)
                gather_rows(rows[:, :], pos_one[:, :]).then_inc(rows_in, 16)

            def x_root(t):
                pool.wait_ge(x_st3, t + 1)
                nc.gpsimd.tensor_tensor(x_rstd[:, :], x_var[:, :], half[:, 0:1], ALU.pow).then_inc(x_st4, 1)

            def f_root(f, b):
                pool.wait_ge(f_st3, f + 1)
                nc.gpsimd.tensor_tensor(b.rstd, b.var, half[:, 0:1], ALU.pow).then_inc(f_st4, 1)

            def add_bias(f, place):
                pool.wait_ge(fn_ok, f + 1)
                nc.gpsimd.tensor_tensor(row(acc, place), row(acc, place), bias_b[:, :], ALU.add).then_inc(biased, 1)

            def xs_lo_split(f, b):
                pool.wait_ge(xs_h, f + 1)
                nc.gpsimd.tensor_tensor(b.xs_lo, b.tile_T, b.xs_hi.bitcast(F32), ALU.subtract).then_inc(xs_l, 1)

            def add_residual(f, place, b):
                wait_alone(pool, y_mul, f + 1)
                nc.gpsimd.tensor_tensor(b.y, b.y, row(acc, place), ALU.add).then_inc(y_ok, 1)

            def slot(s):
                t, f, residual = jobs_of(s)
                if s.intake:
                    gather(t[0])
                    x_root(t[0])
                if s.ffn:
                    f_root(f[0], in_slot)
                if s.proj:
                    for n in range(3):
                        split_lo(s, n)
                if s.ffn:
                    add_bias(*f)
                if s.proj:
                    for n in range(3, 7):
                        split_lo(s, n)
                if s.first_proj:
                    wait_alone(pool, rows_tr, PAIRS)
                    nc.gpsimd.memset(scores[:, :, :], MASKED).then_inc(fill_ok, 1)
                if s.ffn:
                    xs_lo_split(f[0], in_slot)
                if s.proj:
                    for n in range(7, CH):
                        split_lo(s, n)
                if s.ffn:
                    add_residual(*f, in_slot)
                if s.number == 1:
                    pool.wait_ge(bias_in, 16)
                if s.new_mask:
                    wait_alone(pool, shifted, s.U * PAIRS)
                    nc.gpsimd.memset(scores[:, :, :], MASKED).then_inc(fill_ok, 1)
                if s.number == SLOTS:
                    for n in range(HG):
                        split_lo(s, n)

            def last_step(s, step, p):
                f, place, b = last_tile(p)
                if step == 0 and p == 0:
                    wait_alone(pool, roped, SLOTS * KQ)
                    nc.gpsimd.memset(swp[:, 0, :], 0.0).then_inc(route_ok, 1)
                if step == 0:
                    f_root(f, b)
                if step == 1:
                    add_bias(f, place)
                if step == 5:
                    xs_lo_split(f, b)
                if step == 6:
                    add_residual(f, place, b)

            run_slots(pool, slot, last_step)

        @block.scalar
        def _(act):
            def copy(dst, src):
                return nc.scalar.activation(dst, src, ACT.Copy)

            def split_hi(s, n):
                c = STREAM[n] if s.proj else PROJ + n
                r = n % RING
                act.wait_ge(raw_in[r], 16 * ((CH // RING) * s.U + n // RING + 1))
                if c < PROJ:
                    if not (s.first_proj and c < WRING):
                        act.wait_ge(proj_done, s.U * PROJ + c - WRING + 1)
                    hi = flat(w_hi[:, c % WRING, :, :])
                else:
                    if s.wo:
                        act.wait_ge(outproj_done, (s.U - 1) * PAIRS)
                    hi = wo_hi[:, c - PROJ, :]
                copy(hi, raw[:, r, :]).then_inc(wsplit_hi, 1)

            def v_in_rows(s):
                act.wait_ge(v_tr, s.U)
                if not s.first_attn:
                    act.wait_ge(pv_done, (s.U - 1) * PAIRS)
                copy(flat2(v_hi), tr_ps[:, :]).then_inc(v_h, 1)

            def exp_pair(s, p):
                act.wait_ge(shifted, (s.U - 1) * PAIRS + p + 1)
                e = probs[:, p % 2, :, :, :].rearrange("p a b t -> p (a b t)")
                nc.scalar.activation(e, e, ACT.Exp, scale=SCALE).then_inc(exped, 1)

            def pT_hi_split(s, p):
                n = (s.U - 1) * PAIRS + p
                act.wait_ge(probs_tr, n + 1)
                if not (s.first_attn and p == 0):
                    act.wait_ge(pv_done, n)
                copy(pT_hi[0:S, 0, :], tr_ps[0:S, 0:2 * P])
                copy(pT_hi[S:P, 1, :], tr_ps[S:P, 0:2 * P]).then_inc(pT_h, 1)

            def out_hi(s, p):
                act.wait_ge(pv_done, (s.U - 1) * PAIRS + p + 1)
                if not s.first_attn:
                    act.wait_ge(outproj_done, (s.U - 2) * PAIRS + p + 1)
                copy(oT_hi[:, p, :, :].rearrange("p h (b s) -> p b h s", b=2),
                     o_ps[p % 2][:, :].rearrange("p (b h s) -> p b h s", b=2, h=HG)).then_inc(o_hi, 1)

            def swap(s, j):
                bank = chunk[PROJ_BANK[j]]
                act.wait_ge(proj_done, s.U * PROJ + j + 1)
                if j >= 2:
                    act.wait_ge(roped, s.U * KQ + j - 1)
                elif not s.first_proj:
                    act.wait_ge(roped, s.U * KQ - j)
                b = swp[:, j % 2, :]
                copy(b[0:D // 2, :], bank[D // 2:D, :])
                copy(b[D // 2:D, :], bank[0:D // 2, :]).then_inc(swapped, 1)

            def v_out(s):
                act.wait_ge(proj_done, (s.U + 1) * PROJ)
                if s.first_proj:
                    act.wait_ge(sc_lo, 2)
                else:
                    act.wait_ge(v_tr, s.U)
                copy(vT[:, :], chunk[PROJ_BANK[PROJ - 1]][:, :]).then_inc(vT_ok, 1)

            def c_split(t, place):
                act.wait_ge(c_tr, t + 1)
                copy(cT_hi[:, :, span(place * P, P)], by_chunk(aux)).then_inc(c_hi, 1)

            def rope_tables(t, place):
                act.wait_ge(rows_tr, t + 1)
                copy(cosT[:, span(place * P, P)], aux[:, 0:P])
                copy(sinT[:, span(place * P, P)], aux[:, P:2 * P]).then_inc(rope_ok, 1)

            def x_split(t, place):
                act.wait_ge(x_tr, t + 1)
                copy(xT_hi[:, :, span(place * P, P)], by_chunk(aux)).then_inc(x_hi, 1)

            def f_transposed(f, b):
                act.wait_ge(fn_tr, f + 1)
                copy(b.tile_T, b.bank).then_inc(fn_T, 1)

            def router_exp(f, b):
                act.wait_ge(rm_ok, f + 1)
                nc.scalar.activation(b.rexp, b.bank[:, 0:NE], ACT.Exp, bias=b.rmax, accum_out=b.rsum).then_inc(re_ok, 1)

            def route_hi(f, b):
                act.wait_ge(rt_tr, f + 1)
                copy(b.routeT, b.bank[:, 0:P]).then_inc(rt_hi, 1)

            def xs_split(f, b):
                act.wait_ge(xs_ok, f + 1)
                copy(b.xs_hi, b.tile_T).then_inc(xs_h, 1)

            def out_scales(f, b):
                act.wait_ge(osc_done, f + 1)
                if b is in_slot:
                    act.wait_ge(out_done, 16 * (f + 1))
                copy(b.y, b.bank).then_inc(osc_ok, 1)

            def store(f, b):
                act.wait_ge(y_ok, f + 1)
                nc.scalar.dma_start(row_of(out_t, f), b.y).then_inc(out_done, 16)

            def load_residual(t, place):
                nc.scalar.dma_start(row(acc, place), row_of(x_t, t)).then_inc(res_in, 16)

            def slot(s):
                t, f, residual = jobs_of(s)
                if s.attn:
                    v_in_rows(s)
                if s.proj and not s.first_proj:
                    split_hi(s, 0)
                    split_hi(s, 1)
                if s.intake:
                    c_split(*t)
                if s.attn:
                    exp_pair(s, 0)
                if s.proj:
                    split_hi(s, 2)
                if s.intake:
                    rope_tables(*t)
                if s.attn:
                    exp_pair(s, 1)
                if s.ffn:
                    f_transposed(f[0], in_slot)
                if s.attn:
                    pT_hi_split(s, 0)
                if s.intake:
                    x_split(*t)
                if s.attn:
                    exp_pair(s, 2)
                if s.attn:
                    pT_hi_split(s, 1)
                    exp_pair(s, 3)
                if s.ffn:
                    router_exp(f[0], in_slot)
                if s.attn:
                    out_hi(s, 0)
                if s.number == SLOTS:
                    for n in range(HG):
                        split_hi(s, n)
                if s.attn:
                    pT_hi_split(s, 2)
                if s.proj:
                    swap(s, 0)
                if s.attn:
                    out_hi(s, 1)
                if s.proj:
                    split_hi(s, 3)
                    split_hi(s, 4)
                if s.ffn:
                    route_hi(f[0], in_slot)
                if s.attn:
                    pT_hi_split(s, 3)
                if s.proj:
                    swap(s, 1)
                if s.attn:
                    out_hi(s, 2)
                if s.proj:
                    split_hi(s, 5)
                    split_hi(s, 6)
                    swap(s, 2)
                if s.attn:
                    out_hi(s, 3)
                if s.proj:
                    split_hi(s, 7)
                if s.first_proj:
                    ffn_constants()
                if s.ffn:
                    xs_split(f[0], in_slot)
                    out_scales(f[0], in_slot)
                if s.proj:
                    swap(s, 3)
                    split_hi(s, 8)
                    split_hi(s, 9)
                if s.proj:
                    swap(s, 4)
                    v_out(s)
                if s.ffn:
                    store(f[0], in_slot)
                if s.residual:
                    load_residual(*residual)

            def last_step(s, step, p):
                f, _, b = last_tile(p)
                piece = [None, f_transposed, router_exp, route_hi, xs_split, out_scales, None, store][step]
                if piece:
                    piece(f, b)

            def ffn_constants():
                act.wait_ge(gate_tr, 1)
                copy(gateT[:, :, :], by_chunk(GATE_BANK)[:, :, 0:NE]).then_inc(gate_ok, 1)
                act.wait_ge(sc_in, 16 * 6)
                copy(in_sc[:, :], in_raw[:, :]).then_inc(sc_hi, 1)
                copy(out_sc[:, :], out_raw).then_inc(sc_hi, 1)
                for c in range(EC):
                    act.wait_ge(fw_tr, c + 1)
                    copy(sgnT[:, c, :], SGN_BANK[c][:, :]).then_inc(fw_ok, 1)

            def first_quarter():
                for p in range(PAIRS):
                    act.wait_ge(c_tr, p + 1)
                    copy(cT_hi[:, :, bass.ts(p, P)], by_chunk(C_BANK[p])).then_inc(c_hi, 1)
                split_hi(first_slot, 0)
                for p in range(PAIRS):
                    act.wait_ge(x_tr, p + 1)
                    copy(xT_hi[:, :, bass.ts(p, P)], by_chunk(X_BANK[p])).then_inc(x_hi, 1)
                split_hi(first_slot, 1)
                for i in range(PAIRS // 2):
                    act.wait_ge(rows_tr, 2 * i + 2)
                    copy(cosT[:, bass.ts(i, 2 * P)], ROWS_BANK[i][:, 0:2 * P])
                    copy(sinT[:, bass.ts(i, 2 * P)], ROWS_BANK[i][:, 2 * P:4 * P]).then_inc(rope_ok, 2)

            for p in range(PAIRS):
                nc.scalar.dma_start(acc[:, p, :], row_of(x_t, p)).then_inc(x_first_in[p], 16)
            first_slot = Slot(0, 0, False, False)
            first_quarter()
            act.sem_inc(out_done, 16)
            run_slots(act, slot, last_step)
            act.wait_ge(out_done, 16 * (TILES + 1))

        @block.vector
        def _(dve):
            def lo_of(dst, src, hi):
                return nc.vector.tensor_tensor(dst, src, hi.bitcast(F32), ALU.subtract)

            def add_out(s, p):
                dve.wait_ge(outproj_done, (s.U - 2) * PAIRS + p + 1)
                a = row(acc, s.wo_side * PAIRS + p)
                nc.vector.tensor_tensor(a, chunk[OUT_BANK[p]][:, :], a, ALU.add).then_inc(added, 1)

            def soft_a(s, p):
                n = (s.U - 1) * PAIRS + p
                if p == 0 and isinstance(s.g, int) and s.g == 1:
                    dve.wait_ge(mask_in, 32 * (s.q + 1))
                    dve.wait_ge(fill_ok, s.q + 1)
                wait_alone(dve, scores_done, n + 1)
                nc.vector.copy_predicated(
                    scores[:, p, :].rearrange("p (a n) -> p a n", a=2),
                    msk[:, p, :].unsqueeze(1).to_broadcast([P, 2, P]),
                    sc_ps[:, 0:2 * P].rearrange("p (a n) -> p a n", a=2)).then_inc(masked, 1)
                dve.wait_ge(masked, n + 1)
                mx = smax[:, p % 2, :]
                sc = scores[:, p, :].rearrange("p (a t) -> p a t", t=S)
                nc.vector.tensor_reduce(mx, sc, AX.X, ALU.max).then_inc(maxed, 1)
                dve.wait_ge(maxed, n + 1)
                if not (s.first_attn and p < 2):
                    dve.wait_ge(probs_tr, n - 1)
                nc.vector.tensor_tensor(probs[:, p % 2, :, :, :].rearrange("p a b t -> p (a b) t"), sc,
                                        mx.unsqueeze(2).to_broadcast([P, 4, S]), ALU.subtract).then_inc(shifted, 1)

            def soft_b(s, p):
                n = (s.U - 1) * PAIRS + p
                e = probs[:, p % 2, :, :, :].rearrange("p a b t -> p (a b) t")
                dve.wait_ge(exped, n + 1)
                nc.vector.tensor_reduce(ssum[:, p % 2, :], e, AX.X, ALU.add).then_inc(summed, 1)
                dve.wait_ge(summed, n + 1)
                nc.vector.reciprocal(srec[:, p % 2, :], ssum[:, p % 2, :]).then_inc(recd, 1)
                dve.wait_ge(recd, n + 1)
                nc.vector.tensor_tensor(e, e, srec[:, p % 2, :].unsqueeze(2).to_broadcast([P, 4, S]),
                                        ALU.mult).then_inc(probs_ok, 1)

            def v_lo_split(s):
                dve.wait_ge(v_h, s.U)
                lo_of(flat2(v_lo), tr_ps[:, :], flat2(v_hi)).then_inc(v_ok, 1)

            def pT_lo_split(s, p):
                dve.wait_ge(pT_h, (s.U - 1) * PAIRS + p + 1)
                lo_of(pT_lo[0:S, 0, :], tr_ps[0:S, 0:2 * P], pT_hi[0:S, 0, :])
                lo_of(pT_lo[S:P, 1, :], tr_ps[S:P, 0:2 * P], pT_hi[S:P, 1, :]).then_inc(pT_l, 1)

            def out_lo(s, p):
                dve.wait_ge(o_hi, (s.U - 1) * PAIRS + p + 1)
                lo_of(oT_lo[:, p, :, :].rearrange("p h (b s) -> p b h s", b=2),
                      o_ps[p % 2][:, :].rearrange("p (b h s) -> p b h s", b=2, h=HG),
                      oT_hi[:, p, :, :].rearrange("p h (b s) -> p b h s", b=2)).then_inc(o_lo, 1)

            def rotate(s, j):
                n = s.U * KQ + j
                k = j % 2
                here = span(s.side * BT, BT)
                if s.first_proj and j == 0:
                    dve.wait_ge(fw_sgn, EC)
                else:
                    dve.wait_ge(roped, n)
                dve.wait_ge(swapped, n + 1)
                nc.vector.tensor_tensor(rot[:, :], chunk[PROJ_BANK[j]][:, :], cosT[:, here], ALU.mult).then_inc(cos_done, 1)
                nc.vector.tensor_tensor(swp[:, k, :], swp[:, k, :], sinT[:, here], ALU.mult).then_inc(sin_done, 1)
                if s.attn and j == 0:
                    dve.wait_ge(scores_done, s.U * PAIRS)
                dve.wait_ge(cos_done, n + 1)
                dve.wait_ge(sin_done, n + 1)
                if j == 0:
                    dst, a, b = kT[:, :], rot[:, :], swp[:, k, :]
                else:
                    h = j - 1
                    dst = qT[:, h // 2, :].rearrange("p (b a s) -> p b a s", a=2, s=S)[:, :, h % 2, :]
                    a = rot[:, :].rearrange("p (b s) -> p b s", s=S)
                    b = swp[:, k, :].rearrange("p (b s) -> p b s", s=S)
                nc.vector.tensor_tensor(dst, a, b, ALU.add).then_inc(roped, 1)

            def pick_positions(t):
                dve.wait_ge(rows_tr, t)
                nc.vector.tensor_scalar(pos_one[:, :], pos_f[:, one(t)], 0.0, float(MAXPOS - 1), ALU.max, ALU.min).then_inc(pos_ok, 1)

            def tile_stats(src, stat, mv, var, st1, st2, st3, n):
                nc.vector.bn_stats(stat, src).then_inc(st1, 1)
                wait_alone(dve, st1, n + 1)
                nc.vector.bn_aggr(mv, stat).then_inc(st2, 1)
                dve.wait_ge(st2, n + 1)
                nc.vector.tensor_scalar(var, mv[:, 1:2], EPS, None, ALU.add).then_inc(st3, 1)

            def x_stats(t):
                dve.wait_ge(x_in, 16 * (t - PAIRS + 1))
                tile_stats(x_tile[:, :], x_stat[:, :], x_mv[:, :], x_var[:, :], x_st1, x_st2, x_st3, t)

            def x_norm(t):
                dve.wait_ge(x_st4, t + 1)
                nc.vector.tensor_scalar(x_tile[:, :], x_tile[:, :], x_mv[:, 0:1], x_rstd[:, :],
                                        ALU.subtract, ALU.mult).then_inc(xn_ok, 1)

            def c_lo_split(t, place):
                dve.wait_ge(c_hi, t + 1)
                lo_of(cT_lo[:, :, span(place * P, P)], by_chunk(aux), cT_hi[:, :, span(place * P, P)]).then_inc(c_lo, 1)

            def x_lo_split(t, place):
                dve.wait_ge(x_hi, t + 1)
                lo_of(xT_lo[:, :, span(place * P, P)], by_chunk(aux), xT_hi[:, :, span(place * P, P)]).then_inc(x_lo, 1)

            def f_stats(f, place, b):
                tile_stats(row(acc, place), b.stat, b.mv, b.var, f_st1, f_st2, f_st3, f)

            def f_norm(f, place, b):
                dve.wait_ge(f_st4, f + 1)
                nc.vector.tensor_scalar(b.tile, row(acc, place), b.mv[:, 0:1], b.rstd,
                                        ALU.subtract, ALU.mult).then_inc(fn_ok, 1)

            def router_max(f, b):
                dve.wait_ge(lg_done, f + 1)
                nc.vector.tensor_reduce(b.rmax, b.bank[:, 0:NE], AX.X, ALU.max, negate=True).then_inc(rm_ok, 1)

            def routing(f, b):
                dve.wait_ge(re_ok, f + 1)
                nc.vector.reciprocal(b.rrec, b.rsum).then_inc(rr_ok, 1)
                dve.wait_ge(rr_ok, f + 1)
                nc.vector.tensor_scalar(b.route[:, 0:96].rearrange("p (a n) -> p a n", n=32)[:, :, 0:NE],
                                        b.rexp.unsqueeze(1).to_broadcast([P, 3, NE]), b.rrec, None,
                                        ALU.mult).then_inc(rt_ok, 1)

            def route_lo(f, b):
                dve.wait_ge(rt_hi, f + 1)
                lo_of(b.routeT[64:96, :], b.bank[64:96, 0:P], b.routeT[64:96, :]).then_inc(rt_lo, 1)

            def scale_in(f, b):
                dve.wait_ge(isc_done, f + 1)
                nc.vector.tensor_tensor(b.tile_T, b.bank, b.tile_T, ALU.mult).then_inc(xs_ok, 1)

            def finish(f, b):
                dve.wait_ge(f_done, f + 1)
                dve.wait_ge(osc_ok, f + 1)
                nc.vector.tensor_tensor(b.y, b.bank, b.y, ALU.mult).then_inc(y_mul, 1)

            def slot(s):
                t, f, residual = jobs_of(s)
                if s.intake:
                    pick_positions(t[0])
                    x_stats(t[0])
                if s.ffn:
                    dve.wait_ge(added, s.q * KVH * PAIRS)
                    f_stats(*f, in_slot)
                if s.wo:
                    add_out(s, 0)
                if s.attn:
                    v_lo_split(s)
                if s.intake:
                    x_norm(t[0])
                    c_lo_split(*t)
                if s.attn:
                    soft_a(s, 0)
                if s.ffn:
                    f_norm(*f, in_slot)
                if s.wo:
                    add_out(s, 1)
                if s.attn:
                    soft_b(s, 0)
                    soft_a(s, 1)
                if s.wo:
                    add_out(s, 2)
                if s.attn:
                    soft_b(s, 1)
                    soft_a(s, 2)
                    pT_lo_split(s, 0)
                if s.intake:
                    x_lo_split(*t)
                if s.wo:
                    add_out(s, 3)
                if s.attn:
                    soft_b(s, 2)
                    soft_a(s, 3)
                if s.ffn:
                    router_max(f[0], in_slot)
                if s.attn:
                    pT_lo_split(s, 1)
                    soft_b(s, 3)
                if s.ffn:
                    routing(f[0], in_slot)
                if s.attn:
                    out_lo(s, 0)
                    pT_lo_split(s, 2)
                if s.first_proj:
                    ffn_constants()
                if s.proj:
                    rotate(s, 0)
                if s.attn:
                    out_lo(s, 1)
                if s.ffn:
                    route_lo(f[0], in_slot)
                if s.attn:
                    pT_lo_split(s, 3)
                if s.proj:
                    rotate(s, 1)
                if s.attn:
                    out_lo(s, 2)
                if s.ffn:
                    scale_in(f[0], in_slot)
                if s.proj:
                    rotate(s, 2)
                if s.first_proj:
                    scales_lo()
                if s.attn:
                    out_lo(s, 3)
                if s.proj:
                    rotate(s, 3)
                if s.ffn:
                    finish(f[0], in_slot)
                if s.proj:
                    rotate(s, 4)
                if isinstance(s.g, int) and s.g == 1 and s.proj and s.number != 1:
                    wait_alone(dve, res_in, 16 * PAIRS * s.q)

            def last_step(s, step, p):
                f, place, b = last_tile(p)
                if step == 0:
                    add_out(s, p)
                    dve.wait_ge(added, (s.U - 2) * PAIRS + p + 1)
                    f_stats(f, place, b)
                    if p == 0:
                        dve.wait_ge(route_ok, 1)
                    f_norm(f, place, b)
                if step == 2:
                    router_max(f, b)
                    routing(f, b)
                if step == 3:
                    route_lo(f, b)
                if step == 4:
                    scale_in(f, b)
                if step == 6:
                    finish(f, b)

            def first_positions():
                dve.wait_ge(pos_in, 16)
                nc.vector.tensor_copy(pos_f[:, :], pos_i[:, :]).then_inc(pos1, 1)
                dve.wait_ge(pos1, 1)
                nc.vector.tensor_scalar(pos_w[:, :], pos_f[:, :], 0.0, float(MAXPOS), ALU.is_lt, ALU.mult).then_inc(pos2, 1)
                dve.wait_ge(pos2, 1)
                nc.vector.tensor_tensor(pos_f[:, :], pos_f[:, :], pos_w[:, :], ALU.add).then_inc(pos1, 1)
                dve.wait_ge(pos1, 2)
                nc.vector.tensor_scalar(pos_first[:, :], pos_f[:, 0:PAIRS], 0.0, float(MAXPOS - 1),
                                        ALU.max, ALU.min).then_inc(pos_first_ok, 1)
                dve.sem_inc(pos_ok, PAIRS)

            def first_quarter():
                for p in range(PAIRS):
                    dve.wait_ge(x_first_in[p], 16)
                    nc.vector.bn_stats(s_stat[:, p, :], acc[:, p, :]).then_inc(x_st1, 1)
                    dve.wait_ge(c_hi, p + 1)
                    here = bass.ts(p, P)
                    lo_of(cT_lo[:, :, here], by_chunk(C_BANK[p]), cT_hi[:, :, here]).then_inc(c_lo, 1)
                for p in range(PAIRS):
                    dve.wait_ge(x_st1, p + 1)
                    nc.vector.bn_aggr(s_mv[:, p, :], s_stat[:, p, :]).then_inc(x_st2, 1)
                dve.wait_ge(x_st2, PAIRS)
                nc.vector.tensor_scalar(s_var[:, :].unsqueeze(2), s_mv[:, :, 1:2], EPS, None, ALU.add).then_inc(x_st3, PAIRS)
                dve.wait_ge(x_st4, PAIRS)
                for p in range(PAIRS):
                    nc.vector.tensor_scalar(x_first[p][:, :], acc[:, p, :], s_mv[:, p, 0:1], s_rstd[:, p:p + 1],
                                            ALU.subtract, ALU.mult).then_inc(xn_ok, 1)
                for p in range(PAIRS):
                    dve.wait_ge(x_hi, p + 1)
                    here = bass.ts(p, P)
                    lo_of(xT_lo[:, :, here], by_chunk(X_BANK[p]), xT_hi[:, :, here]).then_inc(x_lo, 1)

            def ffn_constants():
                dve.wait_ge(fw_in, 16)
                for c in range(EC):
                    if c > 0:
                        dve.wait_ge(fw_sgn, c)
                    nc.vector.tensor_scalar(rot[:, :], fw[:, c, :], 0.0, None, ALU.is_lt).then_inc(fw_neg, 1)
                    dve.wait_ge(fw_neg, c + 1)
                    nc.vector.scalar_tensor_tensor(fw[:, c, :], fw[:, c, :], 0.0, rot[:, :],
                                                   ALU.is_gt, ALU.subtract).then_inc(fw_sgn, 1)

            def scales_lo():
                dve.wait_ge(sc_hi, 2)
                lo_of(in_sc[32:64, :], in_raw[32:64, :], in_sc[32:64, :]).then_inc(sc_lo, 1)
                lo_of(out_sc[32:64, :], out_raw[32:64, :], out_sc[32:64, :]).then_inc(sc_lo, 1)

            first_positions()
            first_quarter()
            run_slots(dve, slot, last_step)

        @block.tensor
        def _(pe):
            def transpose(dst, src):
                return nc.tensor.transpose(dst, src, ident[:, :])

            def transpose_tile(bank, src):
                for c in range(EC):
                    last = transpose(bank[:, bass.ts(c, P)], src[:, bass.ts(c, P)])
                return last

            def split_products(bank, operands):
                last, n = None, len(operands)
                for i, (a_hi, a_lo, b_hi, b_lo) in enumerate(operands):
                    nc.tensor.matmul(bank, a_hi, b_hi, start=i == 0, stop=False)
                    nc.tensor.matmul(bank, a_hi, b_lo, start=False, stop=False)
                    last = nc.tensor.matmul(bank, a_lo, b_hi, start=False, stop=i == n - 1)
                return last

            def out_proj(s, p):
                n = (s.U - 2) * PAIRS + p
                if p == 3:
                    pe.wait_ge(added, n - 2)
                elif s.after_last:
                    pe.wait_ge(added, (s.U - 3) * PAIRS + (4 if p == 0 else p + 1))
                elif p == 0:
                    pe.wait_ge(cos_done, (s.U - 1) * KQ + 3)
                elif p == 1:
                    pe.wait_ge(vT_ok, s.U)
                else:
                    pe.wait_ge(cos_done, (s.U - 1) * KQ + 5)
                if p == 0:
                    pe.wait_ge(wsplit_lo, SLOTS * CH + HG if s.after_last else s.U * CH)
                pe.wait_ge(o_lo, n + 1)
                split_products(chunk[OUT_BANK[p]][:, :],
                               [(oT_hi[:, p, h, :], oT_lo[:, p, h, :], wo_hi[:, h, :], wo_lo[:, h, :])
                                for h in range(HG)]).then_inc(outproj_done, 1)

            def v_rows(s):
                pe.wait_ge(vT_ok, s.U)
                if not s.first_attn:
                    pe.wait_ge(pT_l, (s.U - 1) * PAIRS)
                for p in range(PAIRS):
                    last = transpose(tr_ps[:, bass.ts(p, D)], vT[:, bass.ts(p, P)])
                last.then_inc(v_tr, 1)

            def scores_of(s, p):
                n = (s.U - 1) * PAIRS + p
                pe.wait_ge(roped, s.U * KQ)
                if not (s.first_attn and p == 0):
                    pe.wait_ge(masked, n)
                for hp in range(HG // 2):
                    for b in range(2):
                        at = 2 * p + b
                        last = nc.tensor.matmul(sc_ps[:, bass.ts(2 * hp + b, S)], qT[:, hp, bass.ts(at, P)],
                                                kT[:, bass.ts(at, S)], start=True, stop=True)
                last.then_inc(scores_done, 1)

            def probs_T(s, p):
                n = (s.U - 1) * PAIRS + p
                pe.wait_ge(probs_ok, n + 1)
                if p == 0:
                    pe.wait_ge(v_ok, s.U)
                else:
                    pe.wait_ge(pT_l, n)
                for hp in range(2):
                    last = transpose(tr_ps[:, bass.ts(hp, P)], probs[:, p % 2, hp, :, :].rearrange("p b t -> p (b t)"))
                last.then_inc(probs_tr, 1)

            def values(s, p):
                n = (s.U - 1) * PAIRS + p
                pe.wait_ge(pT_l, n + 1)
                if not (s.first_attn and p < 2):
                    pe.wait_ge(o_lo, n - 1)
                split_products(o_ps[p % 2][:, :], [(v_hi[:, p, :], v_lo[:, p, :], flat2(pT_hi), flat2(pT_lo))]).then_inc(pv_done, 1)

            def project(s, j):
                if s.first_proj and j < 2:
                    pe.wait_ge(c_lo if j == 0 else x_lo, PAIRS)
                if j < 3 and s.wo:
                    pe.wait_ge(added, (s.U - 2) * PAIRS + 2 + j)
                elif j == 0 and not s.first_proj:
                    pe.wait_ge(vT_ok, s.U)
                elif j == 1 and not s.first_proj:
                    pe.wait_ge(cos_done, s.U * KQ)
                elif j == 2 and not s.first_proj:
                    pe.wait_ge(cos_done, (s.U - 1) * KQ + 3)
                elif j >= 3:
                    pe.wait_ge(cos_done, s.U * KQ + [1, 2, 4][j - 3])
                pe.wait_ge(wsplit_lo, s.U * CH + PLACE[j] + 1)
                src_hi, src_lo = (xT_hi, xT_lo) if 0 < j < PROJ - 1 else (cT_hi, cT_lo)
                here = span(s.side * BT, BT)
                split_products(chunk[PROJ_BANK[j]][:, :],
                               [(w_hi[:, j % WRING, c, :], w_lo[:, j % WRING, c, :], src_hi[:, c, here], src_lo[:, c, here])
                                for c in range(EC)]).then_inc(proj_done, 1)

            def t_context(t):
                pe.wait_ge(c_in, 16 * (t - PAIRS + 1))
                transpose_tile(aux, c_tile).then_inc(c_tr, 1)

            def t_rows(t):
                pe.wait_ge(c_lo, t + 1)
                pe.wait_ge(rows_in, 16 * (t - PAIRS + 1))
                transpose(aux[:, 0:P], rows[:, 0:P])
                transpose(aux[:, P:2 * P], rows[:, P:2 * P]).then_inc(rows_tr, 1)

            def t_x(t):
                pe.wait_ge(rope_ok, t + 1)
                pe.wait_ge(xn_ok, t + 1)
                transpose_tile(aux, x_tile).then_inc(x_tr, 1)

            def t_f(f, b):
                pe.wait_ge(fn_ok, f + 1)
                transpose_tile(b.bank, b.tile).then_inc(fn_tr, 1)

            def t_logits(f, b):
                pe.wait_ge(fn_T, f + 1)
                for c in range(EC):
                    last = nc.tensor.matmul(b.bank[:, 0:NE], b.tile_T[:, bass.ts(c, P)], gateT[:, c, :],
                                            start=c == 0, stop=c == EC - 1)
                last.then_inc(lg_done, 1)

            def t_route(f, b):
                pe.wait_ge(rt_ok, f + 1)
                transpose(b.bank[:, 0:P], b.route).then_inc(rt_tr, 1)

            def t_in_scales(f, b):
                pe.wait_ge(rt_lo, f + 1)
                for c in range(EC):
                    last = nc.tensor.matmul(b.bank[:, bass.ts(c, P)], in_sc[:, bass.ts(c, P)], b.routeT,
                                            start=True, stop=True)
                last.then_inc(isc_done, 1)

            def t_out_scales(f, b):
                pe.wait_ge(xs_ok, f + 1)
                nc.tensor.matmul(b.bank, b.routeT, out_sc[:, :], start=True, stop=True).then_inc(osc_done, 1)

            def t_product(f, b):
                pe.wait_ge(osc_ok, f + 1)
                pe.wait_ge(xs_l, f + 1)
                for c in range(EC):
                    nc.tensor.matmul(b.bank, b.xs_hi[:, bass.ts(c, P)], sgnT[:, c, :], start=c == 0, stop=False)
                    last = nc.tensor.matmul(b.bank, b.xs_lo[:, bass.ts(c, P)], sgnT[:, c, :],
                                            start=False, stop=c == EC - 1)
                last.then_inc(f_done, 1)

            def slot(s):
                if s.number == 1:
                    pe.wait_ge(gate_ok, 1)
                    pe.wait_ge(fw_ok, EC)
                    pe.wait_ge(sc_lo, 2)
                t, f = (job and job[0] for job in jobs_of(s)[:2])
                if s.wo:
                    out_proj(s, 0)
                if s.attn:
                    v_rows(s)
                    scores_of(s, 0)
                if s.intake:
                    t_context(t)
                if s.wo:
                    out_proj(s, 1)
                if s.attn:
                    scores_of(s, 1)
                if s.intake:
                    t_rows(t)
                if s.ffn:
                    t_f(f, in_slot)
                if s.wo:
                    out_proj(s, 2)
                if s.attn:
                    scores_of(s, 2)
                    probs_T(s, 0)
                if s.intake:
                    t_x(t)
                if s.wo:
                    out_proj(s, 3)
                if s.attn:
                    scores_of(s, 3)
                    probs_T(s, 1)
                    values(s, 0)
                if s.ffn:
                    t_logits(f, in_slot)
                if s.proj:
                    project(s, 0)
                if s.attn:
                    probs_T(s, 2)
                    values(s, 1)
                if s.proj:
                    project(s, 1)
                if s.ffn:
                    t_route(f, in_slot)
                if s.attn:
                    probs_T(s, 3)
                    values(s, 2)
                if s.proj:
                    project(s, 2)
                if s.first_proj:
                    ffn_constants()
                if s.ffn:
                    t_in_scales(f, in_slot)
                if s.attn:
                    values(s, 3)
                if s.proj:
                    project(s, 3)
                if s.ffn:
                    t_out_scales(f, in_slot)
                if s.proj:
                    project(s, 4)
                if s.ffn:
                    t_product(f, in_slot)
                if s.proj:
                    project(s, 5)

            def last_step(s, step, p):
                f, _, b = last_tile(p)
                if step == 0:
                    out_proj(s, p)
                elif step < 7:
                    [t_f, t_logits, t_route, t_in_scales, t_out_scales, t_product][step - 1](f, b)

            def first_quarter():
                pe.wait_ge(ident_ok, 2)
                for p in range(PAIRS):
                    pe.wait_ge(c_first_in[p], 16)
                    transpose_tile(C_BANK[p], c_first[:, p, :]).then_inc(c_tr, 1)
                for p in range(PAIRS):
                    pe.wait_ge(xn_ok, p + 1)
                    if p == 3:
                        pe.wait_ge(c_lo, 1)
                    transpose_tile(X_BANK[p], x_first[p]).then_inc(x_tr, 1)
                pe.wait_ge(rows_first_in, 16 * PAIRS)
                for p in range(PAIRS):
                    if p % 2 == 0:
                        pe.wait_ge(c_lo, p // 2 + 2)
                    bank, i = ROWS_BANK[p // 2], p % 2
                    transpose(bank[:, bass.ts(i, P)], rows_first[:, p, 0:P])
                    transpose(bank[:, bass.ts(2 + i, P)], rows_first[:, p, P:2 * P]).then_inc(rows_tr, 1)

            def ffn_constants():
                pe.wait_ge(x_lo, PAIRS)
                pe.wait_ge(rope_ok, PAIRS)
                pe.wait_ge(gate_in, 16)
                transpose_tile(GATE_BANK, gate_raw).then_inc(gate_tr, 1)
                pe.wait_ge(fw_sgn, EC)
                for c in range(EC):
                    for o in range(EC):
                        last = transpose(SGN_BANK[c][:, bass.ts(o, P)], fw[:, o, bass.ts(c, P)])
                    last.then_inc(fw_tr, 1)

            first_quarter()
            run_slots(pe, slot, last_step)


_INS = ["x", "ctx_4096", "pos_BxS2", "mask_BxSxS2_ik0", "L0_xattn_Wq", "L0_xattn_Wk", "L0_xattn_Wv", "L0_xattn_Wo",
        "L0_ffn_weight", "L0_ffn_bias", "L0_ffn_gate_w", "L0_ffn_in_channel_scale", "L0_ffn_out_channel_scale"]


def rope_table(positions=512, dim=128, theta=10000.0):
    import numpy as np
    inv = (1.0 / np.float32(theta) ** (np.arange(0, dim, 2, dtype=np.float32) / np.float32(dim))).astype(np.float32)
    angle = np.arange(positions, dtype=np.float32)[:, None] * inv[None, :]
    c, s = np.cos(angle), np.sin(angle)
    return np.concatenate([c, c, -s, s], axis=1).astype(np.float32)


def kernel(**inputs):
    import numpy as np
    import concourse.bacc as bacc
    from concourse.bass_utils import run_bass_kernel_spmd as run

    nc = bacc.Bacc("TRN2", target_bir_lowering=False, num_devices=1)
    arrays = {f"in_{n}": np.ascontiguousarray(inputs[n]) for n in _INS}
    arrays["rope_table"] = rope_table()
    args = [nc.dram_tensor(n, a.shape, mybir.dt.from_np(a.dtype), kind="ExternalInput").ap() for n, a in arrays.items()]
    shape = arrays["in_x"].shape
    args.append(nc.dram_tensor("result", shape, F32, kind="ExternalOutput").ap())
    attention_ffn(nc, *args)
    r = run(nc, [arrays], core_ids=[0])
    return r.results[0]["result"]
```
